# Optimizing a Trainium2 kernel written in Bass

```python
import numpy as np
import jax
import jax.numpy as jnp

def _softmax(x, axis=-1):
    return jax.nn.softmax(x, axis=axis)

def _gelu(x):
    return jax.nn.gelu(x, approximate=True)

def _silu(x):
    return jax.nn.silu(x)

def _sigmoid(x):
    return jax.nn.sigmoid(x)

def _layernorm(x, axis=-1, eps=1e-05):
    m = jnp.mean(x, axis=axis, keepdims=True)
    v = jnp.var(x, axis=axis, keepdims=True)
    return (x - m) / jnp.sqrt(v + eps)

def _scatter_add(tgt, idx, src, axis=0):
    return tgt.at[idx].add(src)

def _segment_sum(src, seg, n):
    return jax.ops.segment_sum(src, seg, n)
kernel_name = 'mk_xattn_seq_d2_seqx_r4_179072'

def setup_inputs(seed: int=0):
    np.random.seed(seed)
    _w = jnp.asarray

    def _rec_inputs():
        import jax
        import jax.numpy as jnp
        _rk = jax.random.key(seed)
        x = -0.0002928 + 1 * jax.random.normal(jax.random.fold_in(_rk, 1), (4, 512, 512), jnp.float32)
        _lenS = 512 - jax.random.randint(jax.random.fold_in(_rk, 7), (4,), 0, max(1, 512 // 4) + 1, jnp.int32)
        _lenS2 = 512 - jax.random.randint(jax.random.fold_in(_rk, 8), (4,), 0, max(1, 512 // 4) + 1, jnp.int32)
        _ctx_2048P = jax.random.normal(jax.random.fold_in(_rk, 11), (4, 16, 512), jnp.float32)
        _ctx_2048c = jax.random.dirichlet(jax.random.fold_in(_rk, 511), 0.3 * jnp.ones((16,), jnp.float32), (4, 512))
        _ctx_2048t = jnp.einsum('bsk,bkd->bsd', _ctx_2048c, _ctx_2048P)
        _ctx_2048t = _ctx_2048t * jax.lax.rsqrt(jnp.mean(jnp.square(_ctx_2048t)) + 1e-12) * 0.953939
        ctx_2048 = -1.39393e-06 + 0.999914 * (_ctx_2048t + 0.3 * jax.random.normal(jax.random.fold_in(_rk, 611), (4, 512, 512), jnp.float32))
        _validS = jnp.arange(512)[None, :] < _lenS[:, None]
        _validS2 = jnp.arange(512)[None, :] < _lenS2[:, None]
        _causal = jnp.tril(jnp.ones((512, 512), dtype=bool))
        mask_1x1xSxS2_fc1 = jnp.where(jnp.broadcast_to(_validS2[0:1, None, None, :], (1, 1, 512, 512)), 1.0, 0.0).astype(jnp.float32)
        mask_Bx1xSxS2_ff1 = jnp.where(jnp.ones((4, 1, 512, 512), dtype=bool), 1.0, 0.0).astype(jnp.float32)
        mask_BxS2_bf1 = jnp.ones((4, 512), dtype=bool)
        return (x, ctx_2048, mask_1x1xSxS2_fc1, mask_Bx1xSxS2_ff1, mask_BxS2_bf1)
    x, ctx_2048, mask_1x1xSxS2_fc1, mask_Bx1xSxS2_ff1, mask_BxS2_bf1 = _rec_inputs()

    def _L0_xattn_setup():
        import jax, jax.numpy as jnp
        import numpy as np
        H = 512
        NH = 16
        HD = H // NH
        EPS = 1e-05

        def gelu(x):
            return 0.5 * x * (1.0 + jnp.tanh(0.7978845608028654 * x * (1.0 + 0.044715 * x * x)))

        def layernorm(x, scale, bias):
            m = jnp.mean(x, axis=-1, keepdims=True)
            v = jnp.mean(jnp.square(x - m), axis=-1, keepdims=True)
            return (x - m) * jax.lax.rsqrt(v + EPS) * scale + bias

        def split_heads(x):
            b, s, _ = x.shape
            return x.reshape(b, s, NH, HD).transpose(0, 2, 1, 3)

        def merge_heads(x):
            b, nh, s, hd = x.shape
            return x.transpose(0, 2, 1, 3).reshape(b, s, nh * hd)

        def attention(q, k, v, mask):
            scores = jnp.einsum('bhqd,bhkd->bhqk', q, k) / jnp.sqrt(jnp.float32(HD))
            scores = scores * mask - 10000.0 * (1.0 - mask)
            probs = jax.nn.softmax(scores, axis=-1)
            return jnp.einsum('bhqk,bhkd->bhqd', probs, v)
        key = jax.random.key(seed)
        ks = jax.random.split(key, 16)
        b, s, t = (2, 256, 256)
        w = lambda k, i, o: jax.random.normal(k, (i, o), jnp.float32) * 0.02
        inp = {'hidden_states': jax.random.normal(ks[0], (b, s, H), jnp.float32), 'encoder_states': jax.random.normal(ks[1], (b, t, H), jnp.float32), 'ltor_mask': jnp.tril(jnp.ones((1, 1, s, s), jnp.float32)), 'cross_mask': jnp.ones((b, 1, s, t), jnp.float32), 'ln1_s': jnp.ones((H,), jnp.float32), 'ln1_b': jnp.zeros((H,), jnp.float32), 'w_qkv': w(ks[2], H, 3 * H), 'b_qkv': jnp.zeros((3 * H,), jnp.float32), 'w_ao': w(ks[3], H, H), 'b_ao': jnp.zeros((H,), jnp.float32), 'ln2_s': jnp.ones((H,), jnp.float32), 'ln2_b': jnp.zeros((H,), jnp.float32), 'w_q': w(ks[4], H, H), 'b_q': jnp.zeros((H,), jnp.float32), 'w_kv': w(ks[5], H, 2 * H), 'b_kv': jnp.zeros((2 * H,), jnp.float32), 'w_co': w(ks[6], H, H), 'b_co': jnp.zeros((H,), jnp.float32), 'ln3_s': jnp.ones((H,), jnp.float32), 'ln3_b': jnp.zeros((H,), jnp.float32), 'w1': w(ks[7], H, 4 * H), 'b1': jnp.zeros((4 * H,), jnp.float32), 'w2': w(ks[8], 4 * H, H), 'b2': jnp.zeros((H,), jnp.float32)}
        return inp
    _L0_xattn_all = _L0_xattn_setup()
    _L0_xattn_in = {k: v for k, v in _L0_xattn_all.items() if k in ('ln1_s', 'ln1_b', 'w_qkv', 'b_qkv', 'w_ao', 'b_ao', 'ln2_s', 'ln2_b', 'w_q', 'b_q', 'w_kv', 'b_kv', 'w_co', 'b_co', 'ln3_s', 'ln3_b', 'w1', 'b1', 'w2', 'b2')}
    del _L0_xattn_all

    def _L1_xattn_setup():
        import jax, jax.numpy as jnp
        import numpy as np
        D = 512
        H = 16
        HD = D // H
        INNER = 4 * D
        EPS = 1e-05

        def layer_norm(x, w, b):
            mu = jnp.mean(x, axis=-1, keepdims=True)
            var = jnp.mean(jnp.square(x - mu), axis=-1, keepdims=True)
            return (x - mu) * jax.lax.rsqrt(var + EPS) * w + b
        key = jax.random.key(seed)
        ks = jax.random.split(key, 12)
        B, LQ, LK = (4, 256, 512)
        std = 0.02
        inp = {'hidden_states': jax.random.normal(ks[0], (B, LQ, D), jnp.float32), 'encoder_hidden_states': jax.random.normal(ks[1], (B, LK, D), jnp.float32), 'encoder_attention_mask': jnp.ones((B, LK), dtype=bool), 'ln1_w': jnp.ones((D,), jnp.float32), 'ln1_b': jnp.zeros((D,), jnp.float32), 'q_w': jax.random.normal(ks[2], (D, D), jnp.float32) * std, 'q_b': jnp.zeros((D,), jnp.float32), 'k_w': jax.random.normal(ks[3], (D, D), jnp.float32) * std, 'k_b': jnp.zeros((D,), jnp.float32), 'v_w': jax.random.normal(ks[4], (D, D), jnp.float32) * std, 'v_b': jnp.zeros((D,), jnp.float32), 'cproj_w': jax.random.normal(ks[5], (D, D), jnp.float32) * std, 'cproj_b': jnp.zeros((D,), jnp.float32), 'ln2_w': jnp.ones((D,), jnp.float32), 'ln2_b': jnp.zeros((D,), jnp.float32), 'fc_w': jax.random.normal(ks[6], (D, INNER), jnp.float32) * std, 'fc_b': jnp.zeros((INNER,), jnp.float32), 'proj_w': jax.random.normal(ks[7], (INNER, D), jnp.float32) * std, 'proj_b': jnp.zeros((D,), jnp.float32)}
        return inp
    _L1_xattn_all = _L1_xattn_setup()
    _L1_xattn_in = {k: v for k, v in _L1_xattn_all.items() if k in ('ln1_w', 'ln1_b', 'q_w', 'q_b', 'k_w', 'k_b', 'v_w', 'v_b', 'cproj_w', 'cproj_b', 'ln2_w', 'ln2_b', 'fc_w', 'fc_b', 'proj_w', 'proj_b')}
    del _L1_xattn_all
    return {'x': x, 'ctx_2048': ctx_2048, 'mask_1x1xSxS2_fc1': mask_1x1xSxS2_fc1, 'mask_Bx1xSxS2_ff1': mask_Bx1xSxS2_ff1, 'mask_BxS2_bf1': mask_BxS2_bf1, 'L0_xattn_ln1_s': _L0_xattn_in['ln1_s'], 'L0_xattn_ln1_b': _L0_xattn_in['ln1_b'], 'L0_xattn_w_qkv': _L0_xattn_in['w_qkv'], 'L0_xattn_b_qkv': _L0_xattn_in['b_qkv'], 'L0_xattn_w_ao': _L0_xattn_in['w_ao'], 'L0_xattn_b_ao': _L0_xattn_in['b_ao'], 'L0_xattn_ln2_s': _L0_xattn_in['ln2_s'], 'L0_xattn_ln2_b': _L0_xattn_in['ln2_b'], 'L0_xattn_w_q': _L0_xattn_in['w_q'], 'L0_xattn_b_q': _L0_xattn_in['b_q'], 'L0_xattn_w_kv': _L0_xattn_in['w_kv'], 'L0_xattn_b_kv': _L0_xattn_in['b_kv'], 'L0_xattn_w_co': _L0_xattn_in['w_co'], 'L0_xattn_b_co': _L0_xattn_in['b_co'], 'L0_xattn_ln3_s': _L0_xattn_in['ln3_s'], 'L0_xattn_ln3_b': _L0_xattn_in['ln3_b'], 'L0_xattn_w1': _L0_xattn_in['w1'], 'L0_xattn_b1': _L0_xattn_in['b1'], 'L0_xattn_w2': _L0_xattn_in['w2'], 'L0_xattn_b2': _L0_xattn_in['b2'], 'L1_xattn_ln1_w': _L1_xattn_in['ln1_w'], 'L1_xattn_ln1_b': _L1_xattn_in['ln1_b'], 'L1_xattn_q_w': _L1_xattn_in['q_w'], 'L1_xattn_q_b': _L1_xattn_in['q_b'], 'L1_xattn_k_w': _L1_xattn_in['k_w'], 'L1_xattn_k_b': _L1_xattn_in['k_b'], 'L1_xattn_v_w': _L1_xattn_in['v_w'], 'L1_xattn_v_b': _L1_xattn_in['v_b'], 'L1_xattn_cproj_w': _L1_xattn_in['cproj_w'], 'L1_xattn_cproj_b': _L1_xattn_in['cproj_b'], 'L1_xattn_ln2_w': _L1_xattn_in['ln2_w'], 'L1_xattn_ln2_b': _L1_xattn_in['ln2_b'], 'L1_xattn_fc_w': _L1_xattn_in['fc_w'], 'L1_xattn_fc_b': _L1_xattn_in['fc_b'], 'L1_xattn_proj_w': _L1_xattn_in['proj_w'], 'L1_xattn_proj_b': _L1_xattn_in['proj_b']}

def reference(x, ctx_2048, mask_1x1xSxS2_fc1, mask_Bx1xSxS2_ff1, mask_BxS2_bf1, L0_xattn_ln1_s, L0_xattn_ln1_b, L0_xattn_w_qkv, L0_xattn_b_qkv, L0_xattn_w_ao, L0_xattn_b_ao, L0_xattn_ln2_s, L0_xattn_ln2_b, L0_xattn_w_q, L0_xattn_b_q, L0_xattn_w_kv, L0_xattn_b_kv, L0_xattn_w_co, L0_xattn_b_co, L0_xattn_ln3_s, L0_xattn_ln3_b, L0_xattn_w1, L0_xattn_b1, L0_xattn_w2, L0_xattn_b2, L1_xattn_ln1_w, L1_xattn_ln1_b, L1_xattn_q_w, L1_xattn_q_b, L1_xattn_k_w, L1_xattn_k_b, L1_xattn_v_w, L1_xattn_v_b, L1_xattn_cproj_w, L1_xattn_cproj_b, L1_xattn_ln2_w, L1_xattn_ln2_b, L1_xattn_fc_w, L1_xattn_fc_b, L1_xattn_proj_w, L1_xattn_proj_b):
    import jax
    import jax.numpy as jnp

    def _L0_xattn_ref(hidden_states, encoder_states, ltor_mask, cross_mask, ln1_s, ln1_b, w_qkv, b_qkv, w_ao, b_ao, ln2_s, ln2_b, w_q, b_q, w_kv, b_kv, w_co, b_co, ln3_s, ln3_b, w1, b1, w2, b2):
        import jax, jax.numpy as jnp
        import numpy as np
        H = 512
        NH = 16
        HD = H // NH
        EPS = 1e-05

        def gelu(x):
            return 0.5 * x * (1.0 + jnp.tanh(0.7978845608028654 * x * (1.0 + 0.044715 * x * x)))

        def layernorm(x, scale, bias):
            m = jnp.mean(x, axis=-1, keepdims=True)
            v = jnp.mean(jnp.square(x - m), axis=-1, keepdims=True)
            return (x - m) * jax.lax.rsqrt(v + EPS) * scale + bias

        def split_heads(x):
            b, s, _ = x.shape
            return x.reshape(b, s, NH, HD).transpose(0, 2, 1, 3)

        def merge_heads(x):
            b, nh, s, hd = x.shape
            return x.transpose(0, 2, 1, 3).reshape(b, s, nh * hd)

        def attention(q, k, v, mask):
            scores = jnp.einsum('bhqd,bhkd->bhqk', q, k) / jnp.sqrt(jnp.float32(HD))
            scores = scores * mask - 10000.0 * (1.0 - mask)
            probs = jax.nn.softmax(scores, axis=-1)
            return jnp.einsum('bhqk,bhkd->bhqd', probs, v)
        ln_out = layernorm(hidden_states, ln1_s, ln1_b)
        qkv = ln_out @ w_qkv + b_qkv
        q, k, v = jnp.split(qkv, 3, axis=-1)
        ctx = merge_heads(attention(split_heads(q), split_heads(k), split_heads(v), ltor_mask))
        attn_out = ctx @ w_ao + b_ao
        x = hidden_states + attn_out
        ln_out = layernorm(x, ln2_s, ln2_b)
        q = ln_out @ w_q + b_q
        kv = encoder_states @ w_kv + b_kv
        k, v = jnp.split(kv, 2, axis=-1)
        ctx = merge_heads(attention(split_heads(q), split_heads(k), split_heads(v), cross_mask))
        cross_out = ctx @ w_co + b_co
        x = x + cross_out
        ln_out = layernorm(x, ln3_s, ln3_b)
        mlp_out = gelu(ln_out @ w1 + b1) @ w2 + b2
        return x + mlp_out

    def _L1_xattn_ref(hidden_states, encoder_hidden_states, encoder_attention_mask, ln1_w, ln1_b, q_w, q_b, k_w, k_b, v_w, v_b, cproj_w, cproj_b, ln2_w, ln2_b, fc_w, fc_b, proj_w, proj_b):
        import jax, jax.numpy as jnp
        import numpy as np
        D = 512
        H = 16
        HD = D // H
        INNER = 4 * D
        EPS = 1e-05

        def layer_norm(x, w, b):
            mu = jnp.mean(x, axis=-1, keepdims=True)
            var = jnp.mean(jnp.square(x - mu), axis=-1, keepdims=True)
            return (x - mu) * jax.lax.rsqrt(var + EPS) * w + b
        B, LQ, _ = hidden_states.shape
        LK = encoder_hidden_states.shape[1]
        residual = hidden_states
        x = layer_norm(hidden_states, ln1_w, ln1_b)
        q = (x @ q_w + q_b).reshape(B, LQ, H, HD).transpose(0, 2, 1, 3)
        k = (encoder_hidden_states @ k_w + k_b).reshape(B, LK, H, HD).transpose(0, 2, 1, 3)
        v = (encoder_hidden_states @ v_w + v_b).reshape(B, LK, H, HD).transpose(0, 2, 1, 3)
        scale = 1.0 / np.sqrt(HD).astype(np.float32)
        scores = jnp.einsum('bhqd,bhkd->bhqk', q, k) * scale
        mask = encoder_attention_mask[:, None, None, :]
        mask_value = jnp.finfo(scores.dtype).min
        scores = jnp.where(mask, scores, mask_value)
        attn = jax.nn.softmax(scores, axis=-1)
        out = jnp.einsum('bhqk,bhkd->bhqd', attn, v)
        out = out.transpose(0, 2, 1, 3).reshape(B, LQ, D)
        out = out @ cproj_w + cproj_b
        hidden = out + residual
        residual = hidden
        y = layer_norm(hidden, ln2_w, ln2_b)
        y = jax.nn.gelu(y @ fc_w + fc_b, approximate=True)
        y = y @ proj_w + proj_b
        return residual + y
    x = _L0_xattn_ref(x, ctx_2048, mask_1x1xSxS2_fc1, mask_Bx1xSxS2_ff1, L0_xattn_ln1_s, L0_xattn_ln1_b, L0_xattn_w_qkv, L0_xattn_b_qkv, L0_xattn_w_ao, L0_xattn_b_ao, L0_xattn_ln2_s, L0_xattn_ln2_b, L0_xattn_w_q, L0_xattn_b_q, L0_xattn_w_kv, L0_xattn_b_kv, L0_xattn_w_co, L0_xattn_b_co, L0_xattn_ln3_s, L0_xattn_ln3_b, L0_xattn_w1, L0_xattn_b1, L0_xattn_w2, L0_xattn_b2)
    x = _L1_xattn_ref(x, ctx_2048, mask_BxS2_bf1, L1_xattn_ln1_w, L1_xattn_ln1_b, L1_xattn_q_w, L1_xattn_q_b, L1_xattn_k_w, L1_xattn_k_b, L1_xattn_v_w, L1_xattn_v_b, L1_xattn_cproj_w, L1_xattn_cproj_b, L1_xattn_ln2_w, L1_xattn_ln2_b, L1_xattn_fc_w, L1_xattn_fc_b, L1_xattn_proj_w, L1_xattn_proj_b)
    return x

_drawn_inputs = setup_inputs


def setup_inputs(seed=0):
    import zlib

    import numpy as np

    out = dict(_drawn_inputs(seed))
    spreads = {'L0_xattn_ln1_s': (1.0, 0.6),
     'L0_xattn_ln1_b': (0.0, 0.406),
     'L0_xattn_b_qkv': (0.0, 0.1),
     'L0_xattn_b_ao': (0.0, 0.1),
     'L0_xattn_ln2_s': (1.0, 0.6),
     'L0_xattn_ln2_b': (0.0, 0.8),
     'L0_xattn_b_q': (0.0, 2.0),
     'L0_xattn_b_kv': (0.0, 0.1),
     'L0_xattn_b_co': (0.0, 0.1),
     'L0_xattn_ln3_s': (1.0, 0.2),
     'L0_xattn_ln3_b': (0.0, 0.332),
     'L0_xattn_b1': (0.0, 0.1),
     'L0_xattn_b2': (0.0, 0.1),
     'L1_xattn_ln1_w': (1.0, 0.6),
     'L1_xattn_ln1_b': (0.0, 0.8),
     'L1_xattn_q_b': (0.0, 0.8),
     'L1_xattn_k_b': (0.0, 2.0),
     'L1_xattn_v_b': (0.0, 0.1),
     'L1_xattn_cproj_b': (0.0, 0.1),
     'L1_xattn_ln2_w': (1.0, 0.2),
     'L1_xattn_ln2_b': (0.0, 0.355),
     'L1_xattn_fc_b': (0.0, 0.1),
     'L1_xattn_proj_b': (0.0, 0.1)}
    factors = {'L0_xattn_w_q': 7.552, 'L1_xattn_q_w': 7.89, 'L1_xattn_k_w': 7.73}
    for name, (base, spread) in spreads.items():
        noise = np.random.default_rng([zlib.crc32(name.encode()), seed]).standard_normal(out[name].shape)
        drawn = base * np.exp(spread * noise) if base else spread * noise
        out[name] = jnp.asarray(drawn.astype(out[name].dtype))
    for name, factor in factors.items():
        out[name] = (out[name] * factor).astype(out[name].dtype)
    return out
```

```python
import concourse.bass as bass
from concourse import mybir
from contextlib import ExitStack

P = 128
B, S, D = 4, 512, 512
HEADS, HD = 16, 32
HID = 4 * D
KT = D // P
TT = S // P
G = P // HD
NG = HEADS // G
EPS = 1e-5
SCALE = HD ** -0.5
MASKED = 1.7014118346046923e38

ITEMS = NG * TT * G
UNITS = NG * TT
S_BANKS, T_BANKS, U_RING, PT_RING = 3, 2, 4, 6
LAG_T = 2
LAG_AV = LAG_T + 2
LAG_RB = 1
STEPS = ITEMS + 10
UP = HID // 2 // P
SLOTS = 4
RAW = U_RING


def ge(engine, sem, value):
    if isinstance(value, int) and value <= 0:
        return
    engine.wait_ge(sem, value)


def alone(engine, held):
    engine.sem_inc(held, 1)


class Phase:
    pass


class Counts:

    def __init__(self):
        self.at = {}

    def __getitem__(self, name):
        return self.at.get(name, 0)

    def add(self, name, n):
        self.at[name] = self[name] + n


def xattn_program(nc, ins, out):
    f32, f32r, u8 = mybir.dt.float32, mybir.dt.float32r, mybir.dt.uint8
    ACT = mybir.ActivationFunctionType
    ALU = mybir.AluOpType

    x_in = ins["x"].rearrange("b s d -> (b s) d")
    ctx_in = ins["ctx_2048"].rearrange("b s d -> (b s) d")
    out_rows = out.rearrange("b s d -> (b s) d")
    mask_shared = ins["mask_1x1xSxS2_fc1"].rearrange("a b q k -> (a b q) k")
    mask_batch = ins["mask_Bx1xSxS2_ff1"].rearrange("b a q k -> (b a q) k")
    mask_keys = ins["mask_BxS2_bf1"]
    resid = [nc.dram_tensor(f"resid{i}", (B * S, D), f32, kind="Internal").ap() for i in range(6)]

    L0, L1 = "L0_xattn_", "L1_xattn_"

    def cols(name, c):
        return lambda kt: ins[name][kt * P:(kt + 1) * P, c * D:(c + 1) * D]

    def rows(name, c):
        return lambda kt: ins[name][(c * KT + kt) * P:(c * KT + kt + 1) * P, :]

    phases = []

    def attention_phase(kind, src, dst, weights, ln, bq, bk, bv, bo):
        ph = Phase()
        ph.kind, ph.src, ph.dst, ph.weights = kind, src, dst, weights
        ph.ln, ph.bq, ph.bk, ph.bv, ph.out_bias = ln, bq, bk, bv, bo
        ph.attention, ph.cross = True, kind != "self"
        ph.tiles = 2 * TT if ph.cross else TT
        ph.pro_jobs = ph.tiles + 3
        ph.resid_src = src
        phases.append(ph)

    def mlp_phase(half, src, resid_src, dst, weights, ln, b1, b2):
        ph = Phase()
        ph.kind, ph.src, ph.resid_src, ph.dst, ph.weights = "mlp", src, resid_src, dst, weights
        ph.ln, ph.b1, ph.half, ph.out_bias = ln, b1, half, b2
        ph.attention, ph.cross = False, False
        ph.tiles = TT
        ph.pro_jobs = TT
        phases.append(ph)

    attention_phase("self", x_in, resid[0],
                    [cols(L0 + "w_qkv", 0), cols(L0 + "w_qkv", 1), cols(L0 + "w_qkv", 2), cols(L0 + "w_ao", 0)],
                    (L0 + "ln1_s", L0 + "ln1_b"), (L0 + "b_qkv", 0), (L0 + "b_qkv", 4), (L0 + "b_qkv", 8),
                    L0 + "b_ao")
    attention_phase("cross", resid[0], resid[1],
                    [cols(L0 + "w_q", 0), cols(L0 + "w_kv", 0), cols(L0 + "w_kv", 1), cols(L0 + "w_co", 0)],
                    (L0 + "ln2_s", L0 + "ln2_b"), (L0 + "b_q", 0), (L0 + "b_kv", 0), (L0 + "b_kv", 4),
                    L0 + "b_co")
    for h in range(2):
        mlp_phase(h, resid[1], resid[1 + h], resid[2 + h],
                  [cols(L0 + "w1", 2 * h), cols(L0 + "w1", 2 * h + 1), rows(L0 + "w2", 2 * h), rows(L0 + "w2", 2 * h + 1)],
                  (L0 + "ln3_s", L0 + "ln3_b"), L0 + "b1", None if h else L0 + "b2")
    attention_phase("keys", resid[3], resid[4],
                    [cols(L1 + "q_w", 0), cols(L1 + "k_w", 0), cols(L1 + "v_w", 0), cols(L1 + "cproj_w", 0)],
                    (L1 + "ln1_w", L1 + "ln1_b"), (L1 + "q_b", 0), (L1 + "k_b", 0), (L1 + "v_b", 0),
                    L1 + "cproj_b")
    for h in range(2):
        mlp_phase(h, resid[4], resid[4 + h], out_rows if h else resid[5],
                  [cols(L1 + "fc_w", 2 * h), cols(L1 + "fc_w", 2 * h + 1), rows(L1 + "proj_w", 2 * h), rows(L1 + "proj_w", 2 * h + 1)],
                  (L1 + "ln2_w", L1 + "ln2_b"), L1 + "fc_b", None if h else L1 + "proj_b")

    vec_at, vec_cols = {}, 0
    vec_names = []
    for ph in phases:
        names = list(ph.ln) + ([ph.bq[0], ph.bk[0], ph.bv[0]] if ph.attention else [ph.b1])
        for name in names:
            if name not in vec_at:
                vec_at[name] = vec_cols
                vec_names.append(name)
                vec_cols += ins[name].shape[0] // P

    counts = Counts()
    for index, ph in enumerate(phases):
        ph.index = index
        ph.base = dict(counts.at)
        ph.base = {k: counts[k] for k in (
            "job", "dfree", "afree", "x0", "x1", "tile_ln", "item", "tentry", "unit", "group", "qk",
            "enc", "res0", "res1", "store0", "store1", "bias", "mask", "weight", "h")}
        if ph.attention:
            ph.jobs = 3 * (NG - 1) + ph.pro_jobs + TT
            ph.dfrees = ph.jobs
            counts.add("job", B * ph.jobs)
            counts.add("dfree", B * ph.jobs)
            counts.add("item", B * ITEMS)
            counts.add("tentry", B * (ITEMS + NG))
            counts.add("unit", B * UNITS)
            counts.add("group", B * NG)
            counts.add("qk", B * NG)
            counts.add("enc", B * TT * ph.cross)
            counts.add("mask", {"self": TT, "cross": B * TT, "keys": B}[ph.kind])
        else:
            ph.jobs = UP + TT + TT
            ph.dfrees = 2 * TT
            counts.add("job", B * ph.jobs)
            counts.add("dfree", B * ph.dfrees)
            counts.add("afree", B * UP)
            counts.add("h", B * UP)
        counts.add("tile_ln", B * TT)
        for s in range(2):
            counts.add(f"x{s}", B * ph.tiles // 2)
            counts.add(f"res{s}", B * TT // 2)
            counts.add(f"store{s}", B * TT // 2)
        if ph.out_bias:
            counts.add("bias", 1)
        counts.add("weight", SLOTS * KT)
    phase_after = {k: phases[i + 1].base if i + 1 < len(phases) else dict(counts.at) for i, k in enumerate(range(len(phases)))}

    ctx = ExitStack()
    with ctx:
        def sb(name, shape, dt=f32):
            return ctx.enter_context(nc.sbuf_tensor(name, shape, dt))

        def sem(name):
            return ctx.enter_context(nc.semaphore(name))

        w_hi = sb("w_hi", [P, SLOTS, KT, D], f32r)
        w_lo = sb("w_lo", [P, SLOTS, KT, D], f32r)
        xin = sb("xin", [P, 2, D])
        yT_hi = sb("yT_hi", [P, KT, S], f32r)
        yT_lo = sb("yT_lo", [P, KT, S], f32r)
        encT_hi = sb("encT_hi", [P, KT, S], f32r)
        encT_lo = sb("encT_lo", [P, KT, S], f32r)
        q_stack = sb("q_stack", [P, 2, G, S], f32r)
        k_stack = sb("k_stack", [P, 2, G, S], f32r)
        hT_hi = q_stack[:, :, :, :].rearrange("p a g s -> p (a g) s")
        hT_lo = k_stack[:, :, :, :].rearrange("p a g s -> p (a g) s")
        qk_hi = sb("qk_hi", [P, 2, S], f32r)
        qk_lo = sb("qk_lo", [P, 2, S], f32r)
        v_sb = sb("v_sb", [P, 2, TT, P])
        probs = sb("probs", [P, U_RING, S])
        w_raw = probs
        pT = sb("pT", [P, PT_RING, KT, P])
        h32 = pT
        ctx32 = sb("ctx32", [P, S])
        rspread = sb("rspread", [P, S])
        vec_rows = rspread[0:vec_cols, 0:P]
        ctxT_hi = sb("ctxT_hi", [P, KT, S], f32r)
        ctxT_lo = sb("ctxT_lo", [P, KT, S], f32r)
        mask = sb("mask", [P, TT, S])
        maskadd = sb("maskadd", [P, TT, S])
        mask_u8 = mask[:, 0, 0:P].bitcast(u8)
        res = sb("res", [P, 2, D])
        y32 = res[:, :, :].rearrange("p s (k q) -> p s k q", q=P)
        obias = sb("obias", [P, D])
        vecs = sb("vecs", [P, vec_cols])
        ident = sb("ident", [P, P])
        stats = sb("stats", [P, 2, 6])
        moments = sb("moments", [P, 2, 2])
        rstd = sb("rstd", [P, 2, 2])
        minus_half = sb("minus_half", [P, 1])
        rowmin = sb("rowmin", [P, ITEMS])
        rowsum = sb("rowsum", [P, ITEMS])
        rinv = sb("rinv", [P, TT * G])

        bank = [ctx.enter_context(nc.psum_tensor(f"bank{i}", [P, 512], f32)) for i in range(8)]
        score_bank, trans_bank, av_bank, job_bank = bank[0:3], bank[3:5], bank[5], bank[6:8]

        const_done = sem("const_done")
        vec_loaded = sem("vec_loaded")
        vec_turned = sem("vec_turned")
        vec_done = sem("vec_done")
        w_loaded = [sem(f"w_loaded{i}") for i in range(RAW)]
        w_hi_done = sem("w_hi_done")
        w_lo_done = sem("w_lo_done")
        bias_loaded = sem("bias_loaded")
        mask_loaded = sem("mask_loaded")
        mask_done = sem("mask_done")
        x_loaded = [sem(f"x_loaded{i}") for i in range(2)]
        ln_stats = sem("ln_stats")
        ln_mom = sem("ln_mom")
        ln_eps = sem("ln_eps")
        ln_rstd = sem("ln_rstd")
        ln_norm = sem("ln_norm")
        y_done = sem("y_done")
        y_hi_done = sem("y_hi_done")
        y_lo_done = sem("y_lo_done")
        enc_hi_done = sem("enc_hi_done")
        job_done = sem("job_done")
        job_freed = sem("job_freed")
        job_freed_act = sem("job_freed_act")
        qk_hi_done = sem("qk_hi_done")
        stacked = [sem("q_stacked"), sem("k_stacked")]
        scores_done = sem("scores_done")
        scores_read = sem("scores_read")
        rowmin_done = sem("rowmin_done")
        exp_done = sem("exp_done")
        trans_done = sem("trans_done")
        trans_read = sem("trans_read")
        av_done = sem("av_done")
        rinv_done = sem("rinv_done")
        rspread_done = sem("rspread_done")
        ctx_done = sem("ctx_done")
        ctx_hi_done = sem("ctx_hi_done")
        ctx_lo_done = sem("ctx_lo_done")
        h_hi_done = sem("h_hi_done")
        h_lo_done = sem("h_lo_done")
        res_loaded = [sem(f"res_loaded{i}") for i in range(2)]
        res_biased = sem("res_biased")
        stored = [sem(f"stored{i}") for i in range(2)]

        dve_held, pool_held, sp_held = sem("dve_held"), sem("pool_held"), sem("sp_held")

        block = ctx.enter_context(nc.Block())

        def dram_rows(t, b, tt):
            return t[bass.ds(b * S + tt * P, P), :]

        def vec(name, c):
            return vecs[:, vec_at[name] + c:vec_at[name] + c + 1]

        def t_entry(n):
            j = n // (TT * G)
            return n + sum(1 for jj in range(NG) if n > rb_item(jj))

        def rb_item(j):
            return min((j + 1) * TT * G - 1 + LAG_AV - LAG_T, ITEMS - 1)

        def rb_entry(j):
            return rb_item(j) + j + 1

        def av_step(u):
            return G * u + G - 1 + LAG_AV

        def rb_step(j):
            return av_step(TT * (j + 1) - 1)

        def body_loop(engine, body):
            with engine.Fori(0, B - 1) as b:
                body(b, False)
            body(B - 1, True)

        def job_bank_of(k):
            return job_bank[k % 2]

        def pre_at(ph, b):
            return b * ph.jobs, ph.base["job"] + ph.pro_jobs

        @block.sync
        def _(sp):
            def load_tile(ph, src, b, t, tile):
                s = tile % 2
                sp.dma_start(xin[:, s, :], dram_rows(src, b, t)).then_inc(x_loaded[s], 16)

            def prologue_tile(ph, b, rep, k, tile):
                if tile >= 2:
                    ge(sp, job_done, rep + (k + tile - 1))
                    alone(sp, sp_held)
                load_tile(ph, ph.src if tile < TT else ctx_in, b, tile % TT, tile)

            def stack(ph, b, j, which, rep, k):
                st = (q_stack, k_stack)[which]
                sp.wait_ge(job_freed, rep + (k + 1 + ph.base["dfree"] - ph.base["job"]))
                alone(sp, sp_held)
                if j >= 2:
                    sp.wait_ge(scores_done, b * ITEMS + (ph.base["item"] + (j - 1) * TT * G))
                    alone(sp, sp_held)
                places = ((0, qk_hi), (1, qk_lo), (2, qk_hi)) if which == 0 else ((0, qk_hi), (1, qk_hi), (2, qk_lo))
                for g in range(G):
                    for r, part in places:
                        sp.dma_start(st[HD * r:HD * (r + 1), j % 2, g, :].bitcast(f32),
                                     part[HD * g:HD * (g + 1), which, :].bitcast(f32)).then_inc(stacked[which], 16)

            def load_res(ph, b, tt):
                s = tt % 2
                if tt >= 2:
                    sp.wait_ge(stored[s], 16 * (b * (TT // 2) + (ph.base[f"store{s}"] + tt // 2)))
                    alone(sp, sp_held)
                sp.dma_start(res[:, s, :], dram_rows(ph.resid_src, b, tt)).then_inc(res_loaded[s], 16)

            def first_res(ph, b, last):
                sp.wait_ge(y_lo_done, b * TT + (ph.base["tile_ln"] + TT * (1 if last else 2)))
                alone(sp, sp_held)
                load_res(ph, b, 0)
                load_res(ph, b, 1)

            def all_stored(ph, b):
                for s in range(2):
                    sp.wait_ge(stored[s], 16 * (b * (TT // 2) + (ph.base[f"store{s}"] + TT // 2)))
                    alone(sp, sp_held)

            def store(ph, b, tt, rep, k):
                if ph.attention:
                    sp.wait_ge(job_freed, rep + (k + 1 + ph.base["dfree"] - ph.base["job"]))
                    alone(sp, sp_held)
                else:
                    sp.wait_ge(job_freed, k)
                    alone(sp, sp_held)
                sp.dma_start(dram_rows(ph.dst, b, tt), res[:, tt % 2, :]).then_inc(stored[tt % 2], 16)

            def attention_body(ph, b, last):
                rep, k = pre_at(ph, b)
                for n in range(STEPS):
                    j, i = divmod(n, TT * G)
                    if j < NG - 1 and i == 3:
                        stack(ph, b, j + 1, 0, rep, k + 3 * j)
                    if j < NG - 1 and i == 6:
                        stack(ph, b, j + 1, 1, rep, k + 3 * j + 1)
                    if j == NG - 1 and not last:
                        kp = k + 3 * (NG - 1)
                        if i == 0:
                            for tile in range(ph.tiles):
                                prologue_tile(ph, b + 1, rep, kp, tile)
                            first_res(ph, b, False)
                        if i == 15:
                            stack(ph, b + 1, 0, 0, rep, kp + ph.tiles)
                            stack(ph, b + 1, 0, 1, rep, kp + ph.tiles + 1)
                if last:
                    first_res(ph, b, True)
                ko = k + 3 * (NG - 1) + (0 if last else ph.pro_jobs)
                for tt in range(TT):
                    store(ph, b, tt, rep, ko + tt)
                    if tt + 2 < TT:
                        load_res(ph, b, tt + 2)
                all_stored(ph, b)

            def mlp_body(ph, b, last):
                rep, k = pre_at(ph, b)
                if not last:
                    sp.wait_ge(job_done, rep + (k + 1))
                    alone(sp, sp_held)
                    for tile in range(TT):
                        prologue_tile(ph, b + 1, rep, k + UP, tile)
                first_res(ph, b, last)
                for tt in range(TT):
                    store(ph, b, tt, None, b * ph.dfrees + (ph.base["dfree"] + TT * (1 if last else 2) + tt + 1))
                    if tt + 2 < TT:
                        load_res(ph, b, tt + 2)
                all_stored(ph, b)

            for ph in phases:
                for s in range(2):
                    ge(sp, stored[s], 16 * ph.base[f"store{s}"])
                if ph.out_bias:
                    ge(sp, res_biased, (ph.base["bias"]) * B * TT)
                    sp.dma_start(obias[:, :], ins[ph.out_bias].rearrange("(a n) -> a n", a=1).broadcast_to([P, D]))\
                        .then_inc(bias_loaded, 16)
                for tile in range(ph.tiles):
                    prologue_tile(ph, 0, 0, ph.base["job"], tile)
                if ph.attention:
                    stack(ph, 0, 0, 0, 0, ph.base["job"] + ph.tiles)
                    stack(ph, 0, 0, 1, 0, ph.base["job"] + ph.tiles + 1)
                    body_loop(sp, lambda b, last: attention_body(ph, b, last))
                else:
                    body_loop(sp, lambda b, last: mlp_body(ph, b, last))
            for s in range(2):
                sp.wait_ge(stored[s], 16 * counts[f"store{s}"])

        @block.gpsimd
        def _(pool):
            nc.gpsimd.memset(ident[:, :], 0.0).then_inc(const_done, 1)
            nc.gpsimd.memset(minus_half[:, :], -0.5).then_inc(const_done, 1)
            pool.wait_ge(const_done, 2)
            nc.gpsimd.affine_select(out=ident[:, :], in_=ident[:, :], compare_op=ALU.not_equal, fill=1.0, base=0,
                                    pattern=[[-1, P]], channel_multiplier=1).then_inc(const_done, 1)
            for name in vec_names:
                n = ins[name].shape[0] // P
                pool.dma_start(vec_rows[vec_at[name]:vec_at[name] + n, :], ins[name].rearrange("(t p) -> t p", p=P))\
                    .then_inc(vec_loaded, 16)

            def load_weights(ph):
                w0 = ph.base["weight"]

                def fetch(piece):
                    slot, kt = divmod(piece, KT)
                    ge(pool, w_lo_done, w0 + piece - RAW + 1)
                    pool.dma_start(w_raw[:, piece % RAW, :], ph.weights[slot](kt)).then_inc(w_loaded[piece % RAW], 16)

                for piece in range(RAW - 1):
                    fetch(piece)
                for piece in range(SLOTS * KT):
                    slot, kt = divmod(piece, KT)
                    if piece + RAW - 1 < SLOTS * KT:
                        fetch(piece + RAW - 1)
                    pool.wait_ge(w_hi_done, w0 + piece + 1)
                    nc.gpsimd.tensor_tensor(w_lo[:, slot, kt, :], w_raw[:, piece % RAW, :],
                                            w_hi[:, slot, kt, :].bitcast(f32), ALU.subtract).then_inc(w_lo_done, 1)

            def ln_power(ph, b, t):
                n = b * TT + (ph.base["tile_ln"] + t + 1)
                pool.wait_ge(ln_mom, n)
                alone(pool, pool_held)
                nc.gpsimd.tensor_scalar(rstd[:, t % 2, 0:1], moments[:, t % 2, 1:2], EPS, None, ALU.add).then_inc(ln_eps, 1)
                pool.wait_ge(ln_eps, n)
                nc.gpsimd.tensor_tensor(rstd[:, t % 2, 1:2], rstd[:, t % 2, 0:1], minus_half[:, :], ALU.pow).then_inc(ln_rstd, 1)

            def y_low(ph, b, t):
                pool.wait_ge(y_hi_done, b * TT + (ph.base["tile_ln"] + t + 1))
                nc.gpsimd.tensor_tensor(yT_lo[:, :, t * P:(t + 1) * P], y32[:, t % 2, :, :],
                                        yT_hi[:, :, t * P:(t + 1) * P].bitcast(f32), ALU.subtract).then_inc(y_lo_done, 1)

            def spread(ph, b, j):
                group = b * NG + (ph.base["group"] + j)
                pool.wait_ge(rinv_done, group + 1)
                if j >= 1:
                    pool.wait_ge(trans_done, b * (ITEMS + NG) + (ph.base["tentry"] + rb_entry(j - 1) + 1))
                alone(pool, pool_held)
                nc.gpsimd.tensor_copy(rspread[:, :].rearrange("p (n d) -> p n d", d=HD),
                                      rinv[:, :].unsqueeze(2).broadcast_to([P, TT * G, HD])).then_inc(rspread_done, 1)

            def bias_res(ph, b, tt):
                s = tt % 2
                pool.wait_ge(res_loaded[s], 16 * (b * (TT // 2) + (ph.base[f"res{s}"] + tt // 2 + 1)))
                nc.gpsimd.tensor_tensor(res[:, s, :], res[:, s, :], obias[:, :], ALU.add).then_inc(res_biased, 1)

            def load_mask(ph, b):
                m0 = ph.base["mask"]
                if ph.kind == "keys":
                    pool.dma_start(mask_u8, mask_keys[bass.ds(b, 1), :].broadcast_to([P, S])).then_inc(mask_loaded, 16)
                    pool.wait_ge(mask_loaded, 16 * (b + (m0 + 1)))
                    alone(pool, pool_held)
                    nc.gpsimd.tensor_scalar(maskadd[:, 0, :], mask_u8, 1.0, MASKED, ALU.subtract, ALU.mult)\
                        .then_inc(mask_done, 1)
                    return
                src = mask_shared if ph.kind == "self" else mask_batch
                for qt in range(TT):
                    pool.dma_start(mask[:, qt, :], dram_rows(src, b, qt)).then_inc(mask_loaded, 16)
                pool.wait_ge(mask_loaded, 16 * (b * TT + (m0 + TT)))
                alone(pool, pool_held)
                for qt in range(TT):
                    nc.gpsimd.tensor_scalar(maskadd[:, qt, :], mask[:, qt, :], 1.0, -10000.0, ALU.subtract, ALU.mult)\
                        .then_inc(mask_done, 1)

            def attention_body(ph, b, last):
                if ph.kind != "self":
                    ge(pool, rowmin_done, b * ITEMS + ph.base["item"])
                    load_mask(ph, b)
                for n in range(STEPS):
                    if not last and n >= ITEMS - TT * G:
                        i = n - (ITEMS - TT * G)
                        if i < 2 * TT:
                            if i % 2 == 0:
                                ln_power(ph, b + 1, i // 2)
                        if 3 <= i < 3 + 2 * TT and i % 2 == 1:
                            y_low(ph, b + 1, (i - 3) // 2)
                    for j in range(NG):
                        if n == rb_step(j) - 1:
                            spread(ph, b, j)
                for tt in range(TT):
                    bias_res(ph, b, tt)

            def mlp_body(ph, b, last):
                if not last:
                    ln_power(ph, b + 1, 0)
                    ln_power(ph, b + 1, 1)
                for m in range(UP):
                    n = b * UP + (ph.base["h"] + m + 1)
                    pool.wait_ge(h_hi_done, n)
                    nc.gpsimd.tensor_tensor(hT_lo[:, m, :], h32[:, m % 3, :, :].rearrange("p k q -> p (k q)"),
                                            hT_hi[:, m, :].bitcast(f32), ALU.subtract).then_inc(h_lo_done, 1)
                if not last:
                    y_low(ph, b + 1, 0)
                    ln_power(ph, b + 1, 2)
                    y_low(ph, b + 1, 1)
                    ln_power(ph, b + 1, 3)
                    y_low(ph, b + 1, 2)
                    y_low(ph, b + 1, 3)
                if ph.out_bias:
                    for tt in range(TT):
                        bias_res(ph, b, tt)

            for ph in phases:
                ge(pool, job_done, ph.base["job"])
                load_weights(ph)
                if ph.kind == "self":
                    load_mask(ph, 0)
                for t in range(TT):
                    ln_power(ph, 0, t)
                    if t >= 1:
                        y_low(ph, 0, t - 1)
                y_low(ph, 0, TT - 1)
                if ph.out_bias:
                    pool.wait_ge(bias_loaded, 16 * (ph.base["bias"] + 1))
                body_loop(pool, lambda b, last: (attention_body if ph.attention else mlp_body)(ph, b, last))

        @block.tensor
        def _(pe):
            mm = nc.tensor.matmul

            def three(dst, lhs, rhs, first, last):
                mm(dst, lhs[0], rhs[0], start=first, stop=False)
                mm(dst, lhs[0], rhs[1], start=False, stop=False)
                return mm(dst, lhs[1], rhs[0], start=False, stop=last)

            def bank_free(ph, rep, k):
                d = k - 1 + ph.base["dfree"] - ph.base["job"]
                ge(pe, job_freed, rep + d)

            def transposes(k, slot):
                for ft in range(KT):
                    ins_ = nc.tensor.transpose(job_bank_of(k)[:, ft * P:(ft + 1) * P], xin[:, slot, ft * P:(ft + 1) * P],
                                               ident[:, :])
                ins_.then_inc(job_done, 1)

            def ln_job(ph, b, t, k):
                pe.wait_ge(ln_norm, b * TT + (ph.base["tile_ln"] + t + 1))
                transposes(k, t % 2)

            def enc_job(ph, b, t, k):
                s = t % 2
                pe.wait_ge(x_loaded[s], 16 * (b * (ph.tiles // 2) + (ph.base[f"x{s}"] + TT // 2 + t // 2 + 1)))
                transposes(k, s)

            def weights_ready(ph, b, slot):
                if isinstance(b, int):
                    pe.wait_ge(w_lo_done, ph.base["weight"] + KT * (slot + 1))

            def y_ready(ph, b):
                pe.wait_ge(y_lo_done, b * TT + (ph.base["tile_ln"] + TT))

            def qk_job(ph, b, j, which, k):
                hi, lo = (encT_hi, encT_lo) if which and ph.cross else (yT_hi, yT_lo)
                dst = job_bank_of(k)
                c = slice(j * P, (j + 1) * P)
                for kt in range(KT):
                    last = three(dst[:, :], (w_hi[:, which, kt, c], w_lo[:, which, kt, c]),
                                 (hi[:, kt, :], lo[:, kt, :]), kt == 0, kt == KT - 1)
                last.then_inc(job_done, 1)

            def v_job(ph, b, j, k):
                hi, lo = (encT_hi, encT_lo) if ph.cross else (yT_hi, yT_lo)
                dst = job_bank_of(k)
                c = slice(j * P, (j + 1) * P)
                for tt in range(TT):
                    t = slice(tt * P, (tt + 1) * P)
                    for kt in range(KT):
                        last = three(dst[:, t], (hi[:, kt, t], lo[:, kt, t]),
                                     (w_hi[:, 2, kt, c], w_lo[:, 2, kt, c]), kt == 0, kt == KT - 1)
                last.then_inc(job_done, 1)

            def project(ph, b, j, which, rep, k, wb):
                weights_ready(ph, wb, which)
                bank_free(ph, rep, k)
                if which < 2:
                    qk_job(ph, b, j, which, k)
                else:
                    v_job(ph, b, j, k)

            def prologue_tile(ph, b, rep, k, tile):
                bank_free(ph, rep, k + tile)
                if tile < TT:
                    ln_job(ph, b, tile, k + tile)
                else:
                    enc_job(ph, b, tile - TT, k + tile)

            def enc_ready(ph, rep, k):
                pe.wait_ge(job_freed, rep + (k + 1 + ph.base["dfree"] - ph.base["job"]))

            def scores(ph, b, n):
                j, r = divmod(n, TT * G)
                qt, g = divmod(r, G)
                group = b * NG + (ph.base["qk"] + j)
                if r == 0:
                    for which in range(2):
                        pe.wait_ge(stacked[which], 16 * 3 * G * (group + 1))
                if n >= S_BANKS:
                    done = rowmin_done if ph.kind == "keys" else scores_read
                    pe.wait_ge(done, b * ITEMS + (ph.base["item"] + n - S_BANKS + 1))
                mm(score_bank[n % S_BANKS][:, :], q_stack[0:3 * HD, j % 2, g, qt * P:(qt + 1) * P],
                   k_stack[0:3 * HD, j % 2, g, :], start=True, stop=True).then_inc(scores_done, 1)

            def trans_bank_free(ph, b, e):
                if e >= T_BANKS:
                    pe.wait_ge(trans_read, b * (ITEMS + NG) + (ph.base["tentry"] + e - T_BANKS + 1))

            def transpose_item(ph, b, n):
                e = t_entry(n)
                pe.wait_ge(exp_done, b * ITEMS + (ph.base["item"] + n + 1))
                trans_bank_free(ph, b, e)
                for kt in range(KT):
                    last = nc.tensor.transpose(trans_bank[e % T_BANKS][:, kt * P:(kt + 1) * P],
                                               probs[:, n % U_RING, kt * P:(kt + 1) * P], ident[:, :])
                last.then_inc(trans_done, 1)

            def av(ph, b, u):
                j, qt = divmod(u, TT)
                pe.wait_ge(trans_read, b * (ITEMS + NG) + (ph.base["tentry"] + t_entry(G * u + G - 1) + 1))
                if qt == 0 and j > 0:
                    pe.wait_ge(ctx_done, b * NG + (ph.base["group"] + j))
                for kt in range(KT):
                    for g in range(G):
                        last = mm(av_bank[HD * g:HD * (g + 1), qt * P:(qt + 1) * P],
                                  v_sb[:, j % 2, kt, HD * g:HD * (g + 1)],
                                  pT[:, (G * u + g) % PT_RING, kt, :], start=kt == 0, stop=kt == KT - 1)
                last.then_inc(av_done, 1)

            def reciprocals(ph, b, j):
                e = rb_entry(j)
                pe.wait_ge(rspread_done, b * NG + (ph.base["group"] + j + 1))
                trans_bank_free(ph, b, e)
                for qt in range(TT):
                    last = nc.tensor.transpose(trans_bank[e % T_BANKS][:, qt * P:(qt + 1) * P],
                                               rspread[:, qt * P:(qt + 1) * P], ident[:, :])
                last.then_inc(trans_done, 1)

            def out_job(ph, b, tt, rep, k):
                bank_free(ph, rep, k)
                t = slice(tt * P, (tt + 1) * P)
                for kt in range(KT):
                    last = three(job_bank_of(k)[:, :], (ctxT_hi[:, kt, t], ctxT_lo[:, kt, t]),
                                 (w_hi[:, 3, kt, :], w_lo[:, 3, kt, :]), kt == 0, kt == KT - 1)
                last.then_inc(job_done, 1)

            def attention_body(ph, b, last):
                rep, k = pre_at(ph, b)
                kp = k + 3 * (NG - 1)
                for n in range(STEPS):
                    j, i = divmod(n, TT * G)
                    if n < ITEMS:
                        scores(ph, b, n)
                    if 0 <= n - LAG_T < ITEMS:
                        transpose_item(ph, b, n - LAG_T)
                    for u in range(UNITS):
                        if n == av_step(u):
                            if u % TT == 0:
                                jj = u // TT
                                if jj:
                                    pe.wait_ge(job_freed, rep + (k + 3 * (jj - 1) + 3 + ph.base["dfree"] - ph.base["job"]))
                                else:
                                    pe.wait_ge(job_freed, rep + (k + ph.base["dfree"] - ph.base["job"]))
                            av(ph, b, u)
                    for jj in range(NG):
                        if n == rb_step(jj):
                            reciprocals(ph, b, jj)
                    if j < NG - 1 and i in (1, 4, 7):
                        which = (i - 1) // 3
                        project(ph, b, j + 1, which, rep, k + 3 * j + which, None)
                    if j == NG - 1 and not last:
                        if 2 <= i < 2 + 2 * TT and i % 2 == 0:
                            prologue_tile(ph, b + 1, rep, kp, (i - 2) // 2)
                        if ph.cross and 9 <= i < 9 + TT:
                            prologue_tile(ph, b + 1, rep, kp, TT + i - 9)
                        if i == 13:
                            y_ready(ph, b + 1)
                            project(ph, b + 1, 0, 0, rep, kp + ph.tiles, None)
                        if i == 14:
                            if ph.cross:
                                enc_ready(ph, rep, kp + ph.tiles - 1)
                            project(ph, b + 1, 0, 1, rep, kp + ph.tiles + 1, None)
                        if i == 15:
                            project(ph, b + 1, 0, 2, rep, kp + ph.tiles + 2, None)
                ko = kp + (0 if last else ph.pro_jobs)
                weights_ready(ph, 0, 3)
                pe.wait_ge(ctx_lo_done, b * NG + (ph.base["group"] + NG))
                for tt in range(TT):
                    out_job(ph, b, tt, rep, ko + tt)

            def mlp_bank_free(ph, b, l, last):
                p = l - 2
                dbase = ph.base["dfree"] + TT
                if p < 0:
                    pe.wait_ge(job_freed, b * ph.dfrees + (dbase + l - 1))
                elif p < UP:
                    pe.wait_ge(job_freed_act, b * UP + (ph.base["afree"] + p + 1))
                else:
                    pe.wait_ge(job_freed, b * ph.dfrees + (dbase + p - UP + 1))

            def mlp_body(ph, b, last):
                rep, k = pre_at(ph, b)
                y_ready(ph, b)
                for m in range(UP):
                    if m % 4 == 0:
                        weights_ready(ph, 0, m // 4)
                    mlp_bank_free(ph, b, m, last)
                    c = slice((m % 4) * P, (m % 4 + 1) * P)
                    for kt in range(KT):
                        end = three(job_bank_of(k + m)[:, :], (w_hi[:, m // 4, kt, c], w_lo[:, m // 4, kt, c]),
                                    (yT_hi[:, kt, :], yT_lo[:, kt, :]), kt == 0, kt == KT - 1)
                    end.then_inc(job_done, 1)
                l = UP
                if not last:
                    for t in range(TT):
                        mlp_bank_free(ph, b, l, last)
                        ln_job(ph, b + 1, t, k + l)
                        l += 1
                weights_ready(ph, 0, 3)
                pe.wait_ge(h_lo_done, b * UP + (ph.base["h"] + UP))
                for tt in range(TT):
                    mlp_bank_free(ph, b, l, last)
                    t = slice(tt * P, (tt + 1) * P)
                    for m in range(UP):
                        end = three(job_bank_of(k + l)[:, :], (hT_hi[:, m, t], hT_lo[:, m, t]),
                                    (w_hi[:, 2 + m // 4, m % 4, :], w_lo[:, 2 + m // 4, m % 4, :]), m == 0, m == UP - 1)
                    end.then_inc(job_done, 1)
                    l += 1

            pe.wait_ge(const_done, 3)
            pe.wait_ge(vec_loaded, 16 * len(vec_names))
            nc.tensor.transpose(av_bank[:, 0:vec_cols], vec_rows, ident[0:vec_cols, 0:vec_cols]).then_inc(vec_turned, 1)
            for ph in phases:
                k = ph.base["job"]
                for tile in range(ph.tiles):
                    prologue_tile(ph, 0, 0, k, tile)
                if ph.attention:
                    y_ready(ph, 0)
                    project(ph, 0, 0, 0, 0, k + ph.tiles, 0)
                    if ph.cross:
                        enc_ready(ph, 0, k + ph.tiles - 1)
                    project(ph, 0, 0, 1, 0, k + ph.tiles + 1, 0)
                    project(ph, 0, 0, 2, 0, k + ph.tiles + 2, 0)
                body_loop(pe, lambda b, last: (attention_body if ph.attention else mlp_body)(ph, b, last))

        @block.vector
        def _(dve):
            def ln_moments(ph, b, t):
                s = t % 2
                n = b * TT + (ph.base["tile_ln"] + t + 1)
                dve.wait_ge(x_loaded[s], 16 * (b * (ph.tiles // 2) + (ph.base[f"x{s}"] + t // 2 + 1)))
                nc.vector.bn_stats(stats[:, s, :], xin[:, s, :]).then_inc(ln_stats, 1)
                dve.wait_ge(ln_stats, n)
                alone(dve, dve_held)
                nc.vector.bn_aggr(moments[:, s, :], stats[:, s, :]).then_inc(ln_mom, 1)

            def ln_normalise(ph, b, t):
                s = t % 2
                dve.wait_ge(ln_rstd, b * TT + (ph.base["tile_ln"] + t + 1))
                nc.vector.tensor_scalar(xin[:, s, :], xin[:, s, :], moments[:, s, 0:1], rstd[:, s, 1:2],
                                        ALU.subtract, ALU.mult).then_inc(ln_norm, 1)

            def ln_scale(ph, b, t, done, bank_):
                dve.wait_ge(job_done, done)
                if t >= 2:
                    dve.wait_ge(y_lo_done, b * TT + (ph.base["tile_ln"] + t - 1))
                for ft in range(KT):
                    op = nc.vector.tensor_scalar(y32[:, t % 2, ft, :], bank_[:, ft * P:(ft + 1) * P],
                                                 vec(ph.ln[0], ft), vec(ph.ln[1], ft), ALU.mult, ALU.add)
                    if ft == KT - 2:
                        op.then_inc(y_done, 1)
                op.then_inc(job_freed, 1)

            def enc_low(ph, b, t, k):
                dve.wait_ge(enc_hi_done, b * TT + (ph.base["enc"] + t + 1))
                ts = slice(t * P, (t + 1) * P)
                nc.vector.tensor_tensor(encT_lo[:, :, ts], job_bank_of(k)[:, :].rearrange("p (k q) -> p k q", q=P),
                                        encT_hi[:, :, ts].bitcast(f32), ALU.subtract).then_inc(job_freed, 1)

            def qk_low(ph, b, j, which, k):
                name, c = (ph.bq, ph.bk)[which]
                dve.wait_ge(qk_hi_done, 2 * (b * NG + (ph.base["qk"] + j)) + (which + 1))
                nc.vector.scalar_tensor_tensor(out=qk_lo[:, which, :], in0=job_bank_of(k)[:, :], scalar=vec(name, c + j),
                                               in1=qk_hi[:, which, :].bitcast(f32), op0=ALU.add, op1=ALU.subtract)\
                    .then_inc(job_freed, 1)

            def v_copy(ph, b, j, rep, k):
                dve.wait_ge(job_done, rep + (k + 1))
                if j >= 2:
                    dve.wait_ge(av_done, b * UNITS + (ph.base["unit"] + TT * (j - 1)))
                nc.vector.tensor_copy(v_sb[:, j % 2, :, :], job_bank_of(k)[:, :].rearrange("p (t f) -> p t f", f=P))\
                    .then_inc(job_freed, 1)

            def front(ph, b, n):
                item = b * ITEMS + ph.base["item"]
                m_done = ph.base["mask"]
                qt = n // G % TT
                if ph.kind == "keys":
                    if n >= ITEMS:
                        return
                    dve.wait_ge(scores_done, item + (n + 1))
                    if n >= U_RING:
                        dve.wait_ge(trans_done, b * (ITEMS + NG) + (ph.base["tentry"] + t_entry(n - U_RING) + 1))
                    if n == 0:
                        dve.wait_ge(mask_done, b + (m_done + 1))
                    alone(dve, dve_held)
                    nc.vector.tensor_tensor_reduce(out=probs[:, n % U_RING, :], in0=score_bank[n % S_BANKS][:, :],
                                                   in1=maskadd[:, 0, :], scale=-SCALE, scalar=3.0e38, op0=ALU.add,
                                                   op1=ALU.min, accum_out=rowmin[:, n:n + 1]).then_inc(rowmin_done, 1)
                    return
                if n < ITEMS:
                    dve.wait_ge(scores_done, item + (n + 1))
                    if n >= U_RING:
                        dve.wait_ge(trans_done, b * (ITEMS + NG) + (ph.base["tentry"] + t_entry(n - U_RING) + 1))
                    if n == 0:
                        dve.wait_ge(mask_done, m_done + TT if ph.kind == "self" else b * TT + (m_done + TT))
                    if n >= 1:
                        dve.wait_ge(scores_read, item + n)
                    nc.vector.scalar_tensor_tensor(out=probs[:, n % U_RING, :], in0=score_bank[n % S_BANKS][:, :],
                                                   scalar=-SCALE, in1=mask[:, qt, :], op0=ALU.mult, op1=ALU.mult)\
                        .then_inc(scores_read, 1)
                if 1 <= n <= ITEMS:
                    m = n - 1
                    if n == ITEMS:
                        dve.wait_ge(scores_read, item + ITEMS)
                        alone(dve, dve_held)
                    nc.vector.tensor_tensor_reduce(out=probs[:, m % U_RING, :], in0=probs[:, m % U_RING, :],
                                                   in1=maskadd[:, m // G % TT, :], scale=1.0, scalar=3.0e38,
                                                   op0=ALU.add, op1=ALU.min, accum_out=rowmin[:, m:m + 1])\
                        .then_inc(rowmin_done, 1)

            def invert(ph, b, j):
                dve.wait_ge(exp_done, b * ITEMS + (ph.base["item"] + (j + 1) * TT * G))
                if j >= 1:
                    dve.wait_ge(rspread_done, b * NG + (ph.base["group"] + j))
                nc.vector.reciprocal(rinv[:, :], rowsum[:, j * TT * G:(j + 1) * TT * G]).then_inc(rinv_done, 1)

            def normalise(ph, b, j):
                dve.wait_ge(trans_read, b * (ITEMS + NG) + (ph.base["tentry"] + rb_entry(j) + 1))
                dve.wait_ge(av_done, b * UNITS + (ph.base["unit"] + TT * (j + 1)))
                nc.vector.tensor_tensor(ctx32[:, :], av_bank[:, :], ctx32[:, :], ALU.mult).then_inc(ctx_done, 1)

            def ctx_low(ph, b, j):
                name, c = ph.bv
                dve.wait_ge(ctx_hi_done, b * NG + (ph.base["group"] + j + 1))
                nc.vector.scalar_tensor_tensor(out=ctxT_lo[:, j, :], in0=ctx32[:, :], scalar=vec(name, c + j),
                                               in1=ctxT_hi[:, j, :].bitcast(f32), op0=ALU.add, op1=ALU.subtract)\
                    .then_inc(ctx_lo_done, 1)

            def add_residual(ph, b, tt, done, k):
                s = tt % 2
                dve.wait_ge(job_done, done)
                if ph.out_bias:
                    dve.wait_ge(res_biased, b * TT + (ph.base["bias"] * B * TT + tt + 1))
                else:
                    dve.wait_ge(res_loaded[s], 16 * (b * (TT // 2) + (ph.base[f"res{s}"] + tt // 2 + 1)))
                nc.vector.tensor_tensor(res[:, s, :], job_bank_of(k)[:, :], res[:, s, :], ALU.add).then_inc(job_freed, 1)

            def attention_body(ph, b, last):
                rep, k = pre_at(ph, b)
                kp = k + 3 * (NG - 1)
                for n in range(STEPS):
                    j, i = divmod(n, TT * G)
                    front(ph, b, n)
                    if j < NG - 1:
                        if i == 3:
                            qk_low(ph, b, j + 1, 0, k + 3 * j)
                        if i == 6:
                            qk_low(ph, b, j + 1, 1, k + 3 * j + 1)
                        if i == 8:
                            v_copy(ph, b, j + 1, rep, k + 3 * j + 2)
                    for jj in range(NG):
                        if n == rb_step(jj) - 2:
                            invert(ph, b, jj)
                        if n == rb_step(jj) + 2:
                            normalise(ph, b, jj)
                        if n == rb_step(jj) + 3:
                            ctx_low(ph, b, jj)
                    if j == NG - 1 and not last:
                        if i < 2 * TT:
                            if i % 2 == 0:
                                ln_moments(ph, b + 1, i // 2)
                            else:
                                ln_normalise(ph, b + 1, i // 2)
                        if 3 <= i < 3 + 2 * TT and i % 2 == 1:
                            t = (i - 3) // 2
                            ln_scale(ph, b + 1, t, rep + (kp + t + 1), job_bank_of(kp + t))
                        if ph.cross and 10 <= i < 10 + TT:
                            if i == 10:
                                pass
                            enc_low(ph, b + 1, i - 10, kp + TT + i - 10)
                        if i == 15:
                            qk_low(ph, b + 1, 0, 0, kp + ph.tiles)
                    if n == ITEMS and not last:
                        qk_low(ph, b + 1, 0, 1, kp + ph.tiles + 1)
                    if n == ITEMS + 1 and not last:
                        v_copy(ph, b + 1, 0, rep, kp + ph.tiles + 2)
                ko = kp + (0 if last else ph.pro_jobs)
                for tt in range(TT):
                    add_residual(ph, b, tt, rep + (ko + tt + 1), ko + tt)

            def mlp_body(ph, b, last):
                rep, k = pre_at(ph, b)
                l = UP
                if not last:
                    for t in range(2):
                        ln_moments(ph, b + 1, t)
                        ln_normalise(ph, b + 1, t)
                    for t in range(TT):
                        ln_scale(ph, b + 1, t, rep + (k + l + 1), job_bank_of(k + l))
                        if t + 2 < TT:
                            ln_moments(ph, b + 1, t + 2)
                            ln_normalise(ph, b + 1, t + 2)
                        l += 1
                for tt in range(TT):
                    add_residual(ph, b, tt, rep + (k + l + 1), k + l)
                    l += 1

            dve.wait_ge(vec_turned, 1)
            nc.vector.tensor_copy(vecs[:, :], av_bank[:, 0:vec_cols]).then_inc(vec_done, 1)
            dve.wait_ge(vec_done, 1)
            for ph in phases:
                k = ph.base["job"]
                for t in range(TT):
                    ln_moments(ph, 0, t)
                    ln_normalise(ph, 0, t)
                    ln_scale(ph, 0, t, k + t + 1, job_bank_of(k + t))
                if ph.attention:
                    if ph.cross:
                        for t in range(TT):
                            enc_low(ph, 0, t, k + TT + t)
                    qk_low(ph, 0, 0, 0, k + ph.tiles)
                    qk_low(ph, 0, 0, 1, k + ph.tiles + 1)
                    v_copy(ph, 0, 0, 0, k + ph.tiles + 2)
                body_loop(dve, lambda b, last: (attention_body if ph.attention else mlp_body)(ph, b, last))

        @block.scalar
        def _(act):
            def y_high(ph, b, t, freed):
                act.wait_ge(job_freed, freed)
                nc.scalar.activation(yT_hi[:, :, t * P:(t + 1) * P], y32[:, t % 2, :, :], ACT.Copy).then_inc(y_hi_done, 1)

            def enc_high(ph, b, t, rep, k):
                act.wait_ge(job_done, rep + (k + 1))
                nc.scalar.activation(encT_hi[:, :, t * P:(t + 1) * P],
                                     job_bank_of(k)[:, :].rearrange("p (k q) -> p k q", q=P), ACT.Copy)\
                    .then_inc(enc_hi_done, 1)

            def qk_high(ph, b, j, which, rep, k):
                name, c = (ph.bq, ph.bk)[which]
                act.wait_ge(job_done, rep + (k + 1))
                ge(act, stacked[which], 16 * 3 * G * (b * NG + (ph.base["qk"] + j)))
                nc.scalar.activation(qk_hi[:, which, :], job_bank_of(k)[:, :], ACT.Identity, bias=vec(name, c + j))\
                    .then_inc(qk_hi_done, 1)

            def exponent(ph, b, n):
                act.wait_ge(rowmin_done, b * ITEMS + (ph.base["item"] + n + 1))
                nc.scalar.activation(probs[:, n % U_RING, :], probs[:, n % U_RING, :], ACT.Exp, bias=rowmin[:, n:n + 1],
                                     scale=-1.0, accum_out=rowsum[:, n:n + 1]).then_inc(exp_done, 1)

            def copy_item(ph, b, n):
                e = t_entry(n)
                act.wait_ge(trans_done, b * (ITEMS + NG) + (ph.base["tentry"] + e + 1))
                if n >= PT_RING:
                    act.wait_ge(av_done, b * UNITS + (ph.base["unit"] + (n - PT_RING) // G + 1))
                nc.scalar.activation(pT[:, n % PT_RING, :, :].rearrange("p k q -> p (k q)"), trans_bank[e % T_BANKS][:, :],
                                     ACT.Copy).then_inc(trans_read, 1)

            def copy_reciprocals(ph, b, j):
                e = rb_entry(j)
                act.wait_ge(trans_done, b * (ITEMS + NG) + (ph.base["tentry"] + e + 1))
                if j >= 1:
                    act.wait_ge(ctx_lo_done, b * NG + (ph.base["group"] + j))
                nc.scalar.activation(ctx32[:, :], trans_bank[e % T_BANKS][:, :], ACT.Copy).then_inc(trans_read, 1)

            def ctx_high(ph, b, j):
                name, c = ph.bv
                act.wait_ge(ctx_done, b * NG + (ph.base["group"] + j + 1))
                nc.scalar.activation(ctxT_hi[:, j, :], ctx32[:, :], ACT.Identity, bias=vec(name, c + j))\
                    .then_inc(ctx_hi_done, 1)

            def weight_high(ph):
                w0 = ph.base["weight"]
                for piece in range(SLOTS * KT):
                    slot, kt = divmod(piece, KT)
                    act.wait_ge(w_loaded[piece % RAW], 16 * ((w0 + piece) // RAW + 1))
                    nc.scalar.activation(w_hi[:, slot, kt, :], w_raw[:, piece % RAW, :], ACT.Copy).then_inc(w_hi_done, 1)

            def attention_body(ph, b, last):
                rep, k = pre_at(ph, b)
                kp = k + 3 * (NG - 1)
                dd = ph.base["dfree"] - ph.base["job"]
                for n in range(STEPS):
                    j, i = divmod(n, TT * G)
                    if 1 <= n <= ITEMS:
                        exponent(ph, b, n - 1)
                    m = n - LAG_T - 1
                    if 0 <= m < ITEMS:
                        copy_item(ph, b, m)
                    for jj in range(NG):
                        if n == rb_step(jj) + 1:
                            copy_reciprocals(ph, b, jj)
                        if n == rb_step(jj) + 2:
                            ctx_high(ph, b, jj)
                    if j < NG - 1:
                        if i == 2:
                            qk_high(ph, b, j + 1, 0, rep, k + 3 * j)
                        if i == 5:
                            qk_high(ph, b, j + 1, 1, rep, k + 3 * j + 1)
                    if j == NG - 1 and not last:
                        if 3 <= i < 3 + 2 * TT and i % 2 == 1:
                            t = (i - 3) // 2
                            y_high(ph, b + 1, t, rep + (kp + t + 1 + dd))
                        if ph.cross and 9 <= i < 9 + TT:
                            enc_high(ph, b + 1, i - 9, rep, kp + TT + i - 9)
                        if i == 14:
                            qk_high(ph, b + 1, 0, 0, rep, kp + ph.tiles)
                        if i == 15:
                            qk_high(ph, b + 1, 0, 1, rep, kp + ph.tiles + 1)

            def mlp_body(ph, b, last):
                rep, k = pre_at(ph, b)
                freed = b * UP + ph.base["afree"]

                def hidden_high(m):
                    act.wait_ge(job_freed_act, freed + (m + 1))
                    nc.scalar.activation(hT_hi[:, m, :], h32[:, m % 3, :, :].rearrange("p k q -> p (k q)"), ACT.Copy)\
                        .then_inc(h_hi_done, 1)

                for m in range(UP):
                    act.wait_ge(job_done, rep + (k + m + 1))
                    if m >= 3:
                        act.wait_ge(h_lo_done, b * UP + (ph.base["h"] + m - 2))
                    nc.scalar.activation(h32[:, m % 3, :, :].rearrange("p k q -> p (k q)"), job_bank_of(k + m)[:, :],
                                         ACT.Gelu_apprx_tanh, bias=vec(ph.b1, ph.half * UP + m)).then_inc(job_freed_act, 1)
                    if m >= 1:
                        hidden_high(m - 1)
                hidden_high(UP - 1)
                if not last:
                    for t in range(TT):
                        y_high(ph, b + 1, t, b * ph.dfrees + (ph.base["dfree"] + TT + t + 1))

            act.wait_ge(vec_done, 1)
            for ph in phases:
                k = ph.base["job"]
                weight_high(ph)
                for t in range(TT):
                    y_high(ph, 0, t, ph.base["dfree"] + t + 1)
                if ph.attention:
                    if ph.cross:
                        for t in range(TT):
                            enc_high(ph, 0, t, 0, k + TT + t)
                    qk_high(ph, 0, 0, 0, 0, k + ph.tiles)
                    qk_high(ph, 0, 0, 1, 0, k + ph.tiles + 1)
                body_loop(act, lambda b, last: (attention_body if ph.attention else mlp_body)(ph, b, last))


_INS = ['x', 'ctx_2048', 'mask_1x1xSxS2_fc1', 'mask_Bx1xSxS2_ff1', 'mask_BxS2_bf1',
        'L0_xattn_ln1_s', 'L0_xattn_ln1_b', 'L0_xattn_w_qkv', 'L0_xattn_b_qkv', 'L0_xattn_w_ao', 'L0_xattn_b_ao',
        'L0_xattn_ln2_s', 'L0_xattn_ln2_b', 'L0_xattn_w_q', 'L0_xattn_b_q', 'L0_xattn_w_kv', 'L0_xattn_b_kv',
        'L0_xattn_w_co', 'L0_xattn_b_co', 'L0_xattn_ln3_s', 'L0_xattn_ln3_b', 'L0_xattn_w1', 'L0_xattn_b1',
        'L0_xattn_w2', 'L0_xattn_b2', 'L1_xattn_ln1_w', 'L1_xattn_ln1_b', 'L1_xattn_q_w', 'L1_xattn_q_b',
        'L1_xattn_k_w', 'L1_xattn_k_b', 'L1_xattn_v_w', 'L1_xattn_v_b', 'L1_xattn_cproj_w', 'L1_xattn_cproj_b',
        'L1_xattn_ln2_w', 'L1_xattn_ln2_b', 'L1_xattn_fc_w', 'L1_xattn_fc_b', 'L1_xattn_proj_w', 'L1_xattn_proj_b']


def kernel(**inputs):
    import numpy as _np
    import concourse.bacc as _bacc
    from concourse import mybir as _mybir
    from concourse.bass_utils import run_bass_kernel_spmd as _run

    nc = _bacc.Bacc("TRN2", target_bir_lowering=False, num_devices=1)
    arrays, aps = {}, {}
    for name in _INS:
        a = _np.ascontiguousarray(inputs[name])
        arrays[f"in_{name}"] = a
        aps[name] = nc.dram_tensor(f"in_{name}", a.shape, _mybir.dt.from_np(a.dtype), kind="ExternalInput").ap()
    out = nc.dram_tensor("out_0", (B, S, D), _mybir.dt.float32, kind="ExternalOutput").ap()
    xattn_program(nc, aps, out)
    r = _run(nc, [arrays], core_ids=[0])
    return r.results[0]["out_0"]
```

```python
import concourse.bass as bass
from concourse import mybir
from contextlib import ExitStack

P = 128
B, S, D = 4, 512, 512
HEADS, HD = 16, 32
HID = 4 * D
KT = D // P
TT = S // P
G = P // HD
NG = HEADS // G
EPS = 1e-5
SCALE = HD ** -0.5
MASKED = 1.7014118346046923e38

ITEMS = NG * TT * G
S_BANKS, T_BANKS, U_RING, PT_RING = 2, 2, 4, 6
LAG_T = 3
LAG_AV = LAG_T + 2
LAG_NORM = LAG_AV + KT + 1
STEPS = ITEMS + LAG_NORM + 1
UP = HID // 2 // P
SLOTS = 4
RAW = 4
PIECES = SLOTS * KT
PREFETCH = (NG - 2) * TT * G + 13


def ge(engine, sem, value):
    if isinstance(value, int) and value <= 0:
        return
    engine.wait_ge(sem, value)


def alone(engine, held):
    engine.sem_inc(held, 1)


class Phase:
    pass


class Counts:

    def __init__(self):
        self.at = {}

    def __getitem__(self, name):
        return self.at.get(name, 0)

    def add(self, name, n):
        self.at[name] = self[name] + n


def xattn_program(nc, ins, out):
    f32, f32r, u8 = mybir.dt.float32, mybir.dt.float32r, mybir.dt.uint8
    ACT = mybir.ActivationFunctionType
    ALU = mybir.AluOpType

    x_in = ins["x"].rearrange("b s d -> (b s) d")
    ctx_in = ins["ctx_2048"].rearrange("b s d -> (b s) d")
    out_rows = out.rearrange("b s d -> (b s) d")
    mask_shared = ins["mask_1x1xSxS2_fc1"].rearrange("a b q k -> (a b q) k")
    mask_batch = ins["mask_Bx1xSxS2_ff1"].rearrange("b a q k -> (b a q) k")
    mask_keys = ins["mask_BxS2_bf1"]
    resid = [nc.dram_tensor(f"resid{i}", (B * S, D), f32, kind="Internal").ap() for i in range(6)]

    L0, L1 = "L0_xattn_", "L1_xattn_"

    def cols(name, c):
        return lambda kt: ins[name][kt * P:(kt + 1) * P, c * D:(c + 1) * D]

    def rows(name, c):
        return lambda kt: ins[name][(c * KT + kt) * P:(c * KT + kt + 1) * P, :]

    phases = []

    def attention_phase(kind, src, dst, weights, ln, bq, bk, bv, bo):
        ph = Phase()
        ph.kind, ph.src, ph.dst, ph.weights = kind, src, dst, weights
        ph.ln, ph.bq, ph.bk, ph.bv, ph.out_bias = ln, bq, bk, bv, bo
        ph.attention, ph.cross = True, kind != "self"
        ph.tiles = 2 * TT if ph.cross else TT
        ph.pro_jobs = ph.tiles + 3
        ph.resid_src = src
        phases.append(ph)

    def mlp_phase(half, src, resid_src, dst, weights, ln, b1, b2):
        ph = Phase()
        ph.kind, ph.src, ph.resid_src, ph.dst, ph.weights = "mlp", src, resid_src, dst, weights
        ph.ln, ph.b1, ph.half, ph.out_bias = ln, b1, half, b2
        ph.attention, ph.cross = False, False
        ph.tiles = TT
        ph.pro_jobs = TT
        phases.append(ph)

    attention_phase("self", x_in, resid[0],
                    [cols(L0 + "w_qkv", 0), cols(L0 + "w_qkv", 1), cols(L0 + "w_qkv", 2), cols(L0 + "w_ao", 0)],
                    (L0 + "ln1_s", L0 + "ln1_b"), (L0 + "b_qkv", 0), (L0 + "b_qkv", 4), (L0 + "b_qkv", 8),
                    L0 + "b_ao")
    attention_phase("cross", resid[0], resid[1],
                    [cols(L0 + "w_q", 0), cols(L0 + "w_kv", 0), cols(L0 + "w_kv", 1), cols(L0 + "w_co", 0)],
                    (L0 + "ln2_s", L0 + "ln2_b"), (L0 + "b_q", 0), (L0 + "b_kv", 0), (L0 + "b_kv", 4),
                    L0 + "b_co")
    for h in range(2):
        mlp_phase(h, resid[1], resid[1 + h], resid[2 + h],
                  [cols(L0 + "w1", 2 * h), cols(L0 + "w1", 2 * h + 1), rows(L0 + "w2", 2 * h), rows(L0 + "w2", 2 * h + 1)],
                  (L0 + "ln3_s", L0 + "ln3_b"), L0 + "b1", None if h else L0 + "b2")
    attention_phase("keys", resid[3], resid[4],
                    [cols(L1 + "q_w", 0), cols(L1 + "k_w", 0), cols(L1 + "v_w", 0), cols(L1 + "cproj_w", 0)],
                    (L1 + "ln1_w", L1 + "ln1_b"), (L1 + "q_b", 0), (L1 + "k_b", 0), (L1 + "v_b", 0),
                    L1 + "cproj_b")
    for h in range(2):
        mlp_phase(h, resid[4], resid[4 + h], out_rows if h else resid[5],
                  [cols(L1 + "fc_w", 2 * h), cols(L1 + "fc_w", 2 * h + 1), rows(L1 + "proj_w", 2 * h), rows(L1 + "proj_w", 2 * h + 1)],
                  (L1 + "ln2_w", L1 + "ln2_b"), L1 + "fc_b", None if h else L1 + "proj_b")

    vec_at, vec_cols = {}, 0
    vec_names = []
    for ph in phases:
        names = list(ph.ln) + ([ph.bq[0], ph.bk[0], ph.bv[0]] if ph.attention else [ph.b1])
        for name in names:
            if name not in vec_at:
                vec_at[name] = vec_cols
                vec_names.append(name)
                vec_cols += ins[name].shape[0] // P

    counts = Counts()
    names = ("afree", "x0", "x1", "tile_ln", "item", "tentry", "group", "qk", "enc", "res0", "res1",
             "store0", "store1", "bias", "mask", "weight", "h")
    job, dfree = phases[0].pro_jobs, phases[0].pro_jobs
    for index, ph in enumerate(phases):
        ph.index = index
        ph.nxt = phases[index + 1] if index + 1 < len(phases) else None
        ph.base = {k: counts[k] for k in names}
        ph.job0, ph.dfree0 = job, dfree
        nxt_jobs = ph.nxt.pro_jobs if ph.nxt else 0
        if ph.attention:
            ph.jobs = 3 * (NG - 1) + ph.pro_jobs + TT
            ph.dfrees = ph.jobs
            counts.add("item", B * ITEMS)
            counts.add("tentry", B * (ITEMS + NG))
            counts.add("group", B * NG)
            counts.add("qk", B * NG)
            counts.add("enc", B * TT * ph.cross)
            counts.add("mask", {"self": TT, "cross": B * TT, "keys": B}[ph.kind])
        else:
            ph.jobs = UP + TT + TT
            ph.dfrees = 2 * TT
            counts.add("afree", B * UP)
            counts.add("h", B * UP)
        job += B * ph.jobs - ph.pro_jobs + nxt_jobs
        dfree += B * ph.dfrees - ph.pro_jobs + nxt_jobs
        counts.add("tile_ln", B * TT)
        for s in range(2):
            counts.add(f"x{s}", B * ph.tiles // 2)
            counts.add(f"res{s}", B * TT // 2)
            counts.add(f"store{s}", B * TT // 2)
        if ph.out_bias:
            counts.add("bias", 1)
        counts.add("weight", PIECES)

    ctx = ExitStack()
    with ctx:
        def sb(name, shape, dt=f32):
            return ctx.enter_context(nc.sbuf_tensor(name, shape, dt))

        def sem(name):
            return ctx.enter_context(nc.semaphore(name))

        w_hi = sb("w_hi", [P, SLOTS, KT, D], f32r)
        w_lo = sb("w_lo", [P, SLOTS, KT, D], f32r)
        xin = sb("xin", [P, 2, D])
        yT_hi = sb("yT_hi", [P, KT, S], f32r)
        yT_lo = sb("yT_lo", [P, KT, S], f32r)
        encT_hi = sb("encT_hi", [P, KT, S], f32r)
        encT_lo = sb("encT_lo", [P, KT, S], f32r)
        q_stack = sb("q_stack", [P, 2, G, S], f32r)
        k_stack = sb("k_stack", [P, 2, G, S], f32r)
        hT_hi = q_stack[:, :, :, :].rearrange("p a g s -> p (a g) s")
        hT_lo = k_stack[:, :, :, :].rearrange("p a g s -> p (a g) s")
        qk_parts = sb("qk_parts", [P, 2, 2, S])
        qk_hi, qk_lo = qk_parts[:, 0, :, :].bitcast(f32r), qk_parts[:, 1, :, :].bitcast(f32r)
        v_sb = sb("v_sb", [P, 2, TT, P])
        probs = sb("probs", [P, U_RING, S])
        w_raw = probs
        w_raw_qk = qk_parts[:, :, :, :].rearrange("p a b s -> p (a b) s")
        pT = sb("pT", [P, PT_RING, KT, P])
        h32 = pT
        ctx32 = sb("ctx32", [P, S])
        rspread = sb("rspread", [P, S])
        vec_rows = rspread[0:vec_cols, 0:P]
        ctxT_hi = sb("ctxT_hi", [P, KT, S], f32r)
        ctxT_lo = sb("ctxT_lo", [P, KT, S], f32r)
        mask = sb("mask", [P, TT, S])
        maskadd = sb("maskadd", [P, TT, S])
        mask_u8 = mask[:, TT - 1, 0:P].bitcast(u8)
        res = sb("res", [P, 2, D])
        y32_of = {True: res[:, :, :].rearrange("p s (k q) -> p s k q", q=P),
                  False: mask[:, 0:2, :].rearrange("p s (k q) -> p s k q", q=P)}
        obias = sb("obias", [P, D])
        vecs = sb("vecs", [P, vec_cols])
        ident = sb("ident", [P, P])
        stats = sb("stats", [P, 2, 6])
        moments = sb("moments", [P, 2, 2])
        rstd = sb("rstd", [P, 2, 2])
        minus_half = sb("minus_half", [P, 1])
        rowmin = sb("rowmin", [P, ITEMS])
        rowsum = sb("rowsum", [P, ITEMS])
        rinv = sb("rinv", [P, TT * G])

        bank = [ctx.enter_context(nc.psum_tensor(f"bank{i}", [P, 512], f32)) for i in range(8)]
        score_bank, trans_bank, av_bank, job_bank = bank[0:2], bank[2:4], bank[4:6], bank[6:8]

        const_done = sem("const_done")
        vec_loaded = sem("vec_loaded")
        vec_turned = sem("vec_turned")
        vec_done = sem("vec_done")
        w_loaded = [sem(f"w_loaded{i}") for i in range(RAW)]
        w_hi_done = sem("w_hi_done")
        w_lo_done = sem("w_lo_done")
        bias_loaded = sem("bias_loaded")
        mask_loaded = [sem(f"mask_loaded{i}") for i in range(TT)]
        mask_done = sem("mask_done")
        x_loaded = [sem(f"x_loaded{i}") for i in range(2)]
        ln_stats = sem("ln_stats")
        ln_mom = sem("ln_mom")
        ln_eps = sem("ln_eps")
        ln_rstd = sem("ln_rstd")
        ln_norm = sem("ln_norm")
        y_hi_done = sem("y_hi_done")
        y_lo_done = sem("y_lo_done")
        enc_hi_done = sem("enc_hi_done")
        job_done = sem("job_done")
        job_freed = sem("job_freed")
        job_freed_act = sem("job_freed_act")
        qk_hi_done = sem("qk_hi_done")
        stacked = [sem("q_stacked"), sem("k_stacked")]
        scores_done = sem("scores_done")
        scores_read = sem("scores_read")
        rowmin_done = sem("rowmin_done")
        exp_done = sem("exp_done")
        trans_done = sem("trans_done")
        trans_read = sem("trans_read")
        av_done = sem("av_done")
        rinv_done = sem("rinv_done")
        rspread_done = sem("rspread_done")
        ctx_done = sem("ctx_done")
        ctx_hi_done = sem("ctx_hi_done")
        ctx_lo_done = sem("ctx_lo_done")
        h_hi_done = sem("h_hi_done")
        h_lo_done = sem("h_lo_done")
        res_loaded = [sem(f"res_loaded{i}") for i in range(2)]
        res_biased = sem("res_biased")
        stored = [sem(f"stored{i}") for i in range(2)]

        dve_held, pool_held, sp_held = sem("dve_held"), sem("pool_held"), sem("sp_held")

        block = ctx.enter_context(nc.Block())

        def dram_rows(t, b, tt):
            return t[bass.ds(b * S + tt * P, P), :]

        def vec(name, c):
            return vecs[:, vec_at[name] + c:vec_at[name] + c + 1]

        def t_entry(n):
            j = n // (TT * G)
            return n + sum(1 for jj in range(NG) if n > rb_item(jj))

        def rb_item(j):
            return min((j + 1) * TT * G - 1 + LAG_AV - LAG_T, ITEMS - 1)

        def rb_entry(j):
            return rb_item(j) + j + 1

        def rb_step(j):
            return (j + 1) * TT * G - 1 + LAG_AV

        def norm_step(j):
            return (j + 1) * TT * G - 1 + LAG_NORM

        def bodies(engine, ph, body):
            with engine.Fori(0, B - 1) as b:
                body(ph, b, (ph, b + 1))
            body(ph, B - 1, (ph.nxt, 0) if ph.nxt else None)

        def job_bank_of(k):
            return job_bank[k % 2]

        def start(ph, b):
            return b * ph.jobs, ph.job0

        def freed_dd(ph):
            return ph.dfree0 - ph.job0

        def out_place(k, to):
            return k + 3 * (NG - 1) + (to[0].pro_jobs if to else 0)

        def mlp_order(to):
            pro = [("tile", t) for t in range(to[0].tiles)] if to else []
            tail = [("qkv", w) for w in range(3)] if to and to[0].attention else []
            return ([("up", m) for m in range(UP)] + pro[0:2] + [("down", 0), ("down", 1)] + pro[2:4]
                    + [("down", 2), ("down", 3)] + pro[4:] + tail)

        def mlp_freed(ph, b, order, l):
            d0 = b * ph.dfrees
            if l < 0:
                return False, d0 + (ph.dfree0 + l + 1)
            if order[l][0] == "up":
                return True, b * UP + (ph.base["afree"] + l + 1)
            return False, d0 + (ph.dfree0 + sum(1 for kind, _ in order[:l + 1] if kind != "up"))

        def raw_of(ph, piece):
            shared = ph.index and phases[ph.index - 1].attention and piece < 3 * KT
            return (w_raw_qk if shared else w_raw)[:, piece % RAW, :]

        @block.sync
        def _(sp):
            def load_tile(to, tile, rep, before):
                ph, b = to
                if before is not None:
                    sp.wait_ge(job_done, rep + before)
                    alone(sp, sp_held)
                s = tile % 2
                src = ph.src if tile < TT else ctx_in
                sp.dma_start(xin[:, s, :], dram_rows(src, b, tile % TT)).then_inc(x_loaded[s], 16)

            def stack(ph, b, j, which, freed):
                st = (q_stack, k_stack)[which]
                sp.wait_ge(job_freed, freed)
                alone(sp, sp_held)
                places = ((0, qk_hi), (1, qk_lo), (2, qk_hi)) if which == 0 else ((0, qk_hi), (1, qk_hi), (2, qk_lo))
                for g in range(G):
                    for r, part in places:
                        sp.dma_start(st[HD * r:HD * (r + 1), j % 2, g, :].bitcast(f32),
                                     part[HD * g:HD * (g + 1), which, :].bitcast(f32)).then_inc(stacked[which], 16)

            def load_res(ph, b, tt):
                s = tt % 2
                if tt >= 2:
                    sp.wait_ge(stored[s], 16 * (b * (TT // 2) + (ph.base[f"store{s}"] + tt // 2)))
                    alone(sp, sp_held)
                sp.dma_start(res[:, s, :], dram_rows(ph.resid_src, b, tt)).then_inc(res_loaded[s], 16)

            def store(ph, b, tt, freed):
                sp.wait_ge(job_freed, freed)
                alone(sp, sp_held)
                sp.dma_start(dram_rows(ph.dst, b, tt), res[:, tt % 2, :]).then_inc(stored[tt % 2], 16)

            def body_end(ph, b, to):
                for s in range(2):
                    sp.wait_ge(stored[s], 16 * (b * (TT // 2) + (ph.base[f"store{s}"] + TT // 2)))
                    alone(sp, sp_held)
                if to and to[0] is not ph and to[0].out_bias:
                    sp.wait_ge(res_biased, to[0].base["bias"] * B * TT)
                    load_out_bias(to[0])

            def load_out_bias(ph):
                sp.dma_start(obias[:, :], ins[ph.out_bias].rearrange("(a n) -> a n", a=1).broadcast_to([P, D]))\
                    .then_inc(bias_loaded, 16)

            def load_mask(to, qt):
                sp.dma_start(mask[:, qt, :], dram_rows(mask_shared if to[0].kind == "self" else mask_batch, to[1], qt))\
                    .then_inc(mask_loaded[qt], 16)

            def load_keys(to):
                sp.dma_start(mask_u8, mask_keys[bass.ds(to[1], 1), :].broadcast_to([P, S])).then_inc(mask_loaded[TT - 1], 16)

            def attention_body(ph, b, to):
                rep, k = start(ph, b)
                dd = freed_dd(ph)
                kp = k + 3 * (NG - 1)
                ko = out_place(k, to)
                group3 = ITEMS - TT * G
                for n in range(STEPS):
                    j, i = divmod(n, TT * G)
                    for which in range(2):
                        if j < NG - 1 and i == 5 + 4 * which:
                            stack(ph, b, j + 1, which, rep + (k + 3 * j + which + 1 + dd))
                        if to[0].attention and n == ITEMS + 3 + 2 * which:
                            stack(*to, 0, which, rep + (kp + to[0].tiles + which + 1 + dd))
                    for tile, at in zip(range(to[0].tiles), (0, 0, 3, 5, 7, 9, 10, 11)):
                        if n == group3 + at:
                            load_tile(to, tile, rep, None if tile < 2 else kp + tile - 1)
                    for qt in range(TT):
                        if to[0].kind == "cross" and n == group3 + G * qt + 5:
                            sp.wait_ge(scores_read, b * ITEMS + (ph.base["item"] + group3 + G * (qt + 1)))
                            alone(sp, sp_held)
                            load_mask(to, qt)
                    if to[0].kind == "keys" and n == group3 + 5:
                        sp.wait_ge(mask_done, b + (ph.base["mask"] + 1))
                        alone(sp, sp_held)
                        load_keys(to)
                    if n == group3 + 12:
                        sp.wait_ge(y_lo_done, to[1] * TT + (to[0].base["tile_ln"] + TT))
                        alone(sp, sp_held)
                        load_res(ph, b, 0)
                        load_res(ph, b, 1)
                for tt in range(TT):
                    store(ph, b, tt, rep + (ko + tt + 1 + dd))
                    if tt + 2 < TT:
                        load_res(ph, b, tt + 2)
                body_end(ph, b, to)

            def mlp_body(ph, b, to):
                rep, k = start(ph, b)
                order = mlp_order(to)

                def freed(job):
                    return mlp_freed(ph, b, order, order.index(job))[1]

                def tile(t):
                    load_tile(to, t, rep, None if t < 2 else k + order.index(("tile", t - 2)) + 1)

                sp.wait_ge(job_done, rep + (k + 1))
                alone(sp, sp_held)
                if to:
                    tile(0)
                    tile(1)
                    if to[0].kind == "keys":
                        load_keys(to)
                load_res(ph, b, 0)
                load_res(ph, b, 1)
                if to:
                    tile(2)
                    tile(3)
                store(ph, b, 0, freed(("down", 0)))
                load_res(ph, b, 2)
                store(ph, b, 1, freed(("down", 1)))
                load_res(ph, b, 3)
                if to and to[0].cross:
                    tile(4)
                    tile(5)
                store(ph, b, 2, freed(("down", 2)))
                store(ph, b, 3, freed(("down", 3)))
                if to and to[0].cross:
                    tile(6)
                    tile(7)
                    for which in range(2):
                        stack(*to, 0, which, freed(("qkv", which)))
                body_end(ph, b, to)

            first = phases[0]
            load_tile((first, 0), 0, 0, None)
            load_tile((first, 0), 1, 0, None)
            for name in vec_names:
                n = ins[name].shape[0] // P
                sp.dma_start(vec_rows[vec_at[name]:vec_at[name] + n, :], ins[name].rearrange("(t p) -> t p", p=P))\
                    .then_inc(vec_loaded, 16)
            for tile_ in range(2, TT):
                load_tile((first, 0), tile_, 0, tile_ - 1)
            load_out_bias(first)
            for qt in range(TT):
                load_mask((first, 0), qt)
            for which in range(2):
                stack(first, 0, 0, which, first.tiles + which + 1)
            for ph in phases:
                bodies(sp, ph, attention_body if ph.attention else mlp_body)

        @block.gpsimd
        def _(pool):
            nc.gpsimd.memset(ident[:, :], 0.0).then_inc(const_done, 1)
            nc.gpsimd.memset(minus_half[:, :], -0.5).then_inc(const_done, 1)
            pool.wait_ge(const_done, 2)
            nc.gpsimd.affine_select(out=ident[:, :], in_=ident[:, :], compare_op=ALU.not_equal, fill=1.0, base=0,
                                    pattern=[[-1, P]], channel_multiplier=1).then_inc(const_done, 1)
            def weight_low(ph, piece):
                slot, kt = divmod(piece, KT)
                pool.wait_ge(w_hi_done, ph.base["weight"] + piece + 1)
                nc.gpsimd.tensor_tensor(w_lo[:, slot, kt, :], raw_of(ph, piece), w_hi[:, slot, kt, :].bitcast(f32),
                                        ALU.subtract).then_inc(w_lo_done, 1)

            def ln_power(ph, b, t):
                n = b * TT + (ph.base["tile_ln"] + t + 1)
                pool.wait_ge(ln_mom, n)
                alone(pool, pool_held)
                nc.gpsimd.tensor_scalar(rstd[:, t % 2, 0:1], moments[:, t % 2, 1:2], EPS, None, ALU.add).then_inc(ln_eps, 1)
                pool.wait_ge(ln_eps, n)
                nc.gpsimd.tensor_tensor(rstd[:, t % 2, 1:2], rstd[:, t % 2, 0:1], minus_half[:, :], ALU.pow).then_inc(ln_rstd, 1)

            def y_low(ph, b, t, y32):
                pool.wait_ge(y_hi_done, b * TT + (ph.base["tile_ln"] + t + 1))
                nc.gpsimd.tensor_tensor(yT_lo[:, :, t * P:(t + 1) * P], y32[:, t % 2, :, :],
                                        yT_hi[:, :, t * P:(t + 1) * P].bitcast(f32), ALU.subtract).then_inc(y_lo_done, 1)

            def spread(ph, b, j):
                group = b * NG + (ph.base["group"] + j)
                pool.wait_ge(rinv_done, group + 1)
                if j >= 1:
                    pool.wait_ge(trans_done, b * (ITEMS + NG) + (ph.base["tentry"] + rb_entry(j - 1) + 1))
                alone(pool, pool_held)
                nc.gpsimd.tensor_copy(rspread[:, :].rearrange("p (n d) -> p n d", d=HD),
                                      rinv[:, :].unsqueeze(2).broadcast_to([P, TT * G, HD])).then_inc(rspread_done, 1)

            def bias_res(ph, b, tt):
                s = tt % 2
                pool.wait_ge(res_loaded[s], 16 * (b * (TT // 2) + (ph.base[f"res{s}"] + tt // 2 + 1)))
                nc.gpsimd.tensor_tensor(res[:, s, :], res[:, s, :], obias[:, :], ALU.add).then_inc(res_biased, 1)

            def attention_body(ph, b, to):
                for n in range(STEPS):
                    i = n - (ITEMS - TT * G)
                    if i in (0, 2, 4, 6):
                        ln_power(*to, i // 2)
                    if i in (3, 5, 7, 9):
                        y_low(*to, (i - 3) // 2, y32_of[True])
                    for j in range(NG):
                        if n == rb_step(j) - 1:
                            spread(ph, b, j)
                    if to[0] is not ph and 0 <= n - PREFETCH < 3 * KT:
                        weight_low(to[0], n - PREFETCH)
                for tt in range(TT):
                    bias_res(ph, b, tt)
                if to[0] is not ph:
                    for piece in range(3 * KT, PIECES):
                        weight_low(to[0], piece)

            def mlp_body(ph, b, to):
                fresh = to and to[0] is not ph
                if to:
                    ln_power(*to, 0)
                    ln_power(*to, 1)
                if fresh:
                    for piece in range(KT):
                        weight_low(to[0], piece)
                for half in range(2):
                    if to and half:
                        ln_power(*to, 2)
                        ln_power(*to, 3)
                        if fresh:
                            for piece in range(KT, 2 * KT):
                                weight_low(to[0], piece)
                    for t in (2 * half, 2 * half + 1):
                        if to:
                            y_low(*to, t, y32_of[False])
                        if ph.out_bias:
                            bias_res(ph, b, t)
                if fresh:
                    for piece in range(2 * KT, PIECES):
                        weight_low(to[0], piece)

            first = phases[0]
            ln_power(first, 0, 0)
            for t in range(TT):
                if t + 1 < TT:
                    ln_power(first, 0, t + 1)
                for piece in range(t * KT, (t + 1) * KT):
                    weight_low(first, piece)
                y_low(first, 0, t, y32_of[True])
            for ph in phases:
                if ph.out_bias:
                    pool.wait_ge(bias_loaded, 16 * (ph.base["bias"] + 1))
                bodies(pool, ph, attention_body if ph.attention else mlp_body)

        @block.tensor
        def _(pe):
            mm = nc.tensor.matmul

            def three(dst, lhs, rhs, first, last):
                mm(dst, lhs[0], rhs[0], start=first, stop=False)
                mm(dst, lhs[0], rhs[1], start=False, stop=False)
                return mm(dst, lhs[1], rhs[0], start=False, stop=last)

            def bank_free(ph, rep, k):
                ge(pe, job_freed, rep + (k - 1 + freed_dd(ph)))

            def transposes(k, slot):
                for ft in range(KT):
                    ins_ = nc.tensor.transpose(job_bank_of(k)[:, ft * P:(ft + 1) * P], xin[:, slot, ft * P:(ft + 1) * P],
                                               ident[:, :])
                ins_.then_inc(job_done, 1)

            def ln_job(ph, b, t, k):
                pe.wait_ge(ln_norm, b * TT + (ph.base["tile_ln"] + t + 1))
                transposes(k, t % 2)

            def enc_job(ph, b, t, k):
                s = t % 2
                pe.wait_ge(x_loaded[s], 16 * (b * (ph.tiles // 2) + (ph.base[f"x{s}"] + TT // 2 + t // 2 + 1)))
                transposes(k, s)

            def weights_ready(ph, slot):
                pe.wait_ge(w_lo_done, ph.base["weight"] + KT * (slot + 1))

            def y_ready(ph, b):
                pe.wait_ge(y_lo_done, b * TT + (ph.base["tile_ln"] + TT))

            def qk_part(ph, j, which, k, kt):
                hi, lo = (encT_hi, encT_lo) if which and ph.cross else (yT_hi, yT_lo)
                c = slice(j * P, (j + 1) * P)
                return three(job_bank_of(k)[:, :], (w_hi[:, which, kt, c], w_lo[:, which, kt, c]),
                             (hi[:, kt, :], lo[:, kt, :]), kt == 0, kt == KT - 1)

            def v_part(ph, j, k, tt):
                hi, lo = (encT_hi, encT_lo) if ph.cross else (yT_hi, yT_lo)
                c = slice(j * P, (j + 1) * P)
                t = slice(tt * P, (tt + 1) * P)
                for kt in range(KT):
                    last = three(job_bank_of(k)[:, t], (hi[:, kt, t], lo[:, kt, t]),
                                 (w_hi[:, 2, kt, c], w_lo[:, 2, kt, c]), kt == 0, kt == KT - 1)
                return last

            def project(ph, j, which, k, parts=range(KT)):
                for part in parts:
                    last = v_part(ph, j, k, part) if which == 2 else qk_part(ph, j, which, k, part)
                    if part == KT - 1:
                        last.then_inc(job_done, 1)

            def prologue_tile(ph, b, tile, k):
                if tile < TT:
                    ln_job(ph, b, tile, k)
                else:
                    enc_job(ph, b, tile - TT, k)

            def scores(ph, b, n):
                j, r = divmod(n, TT * G)
                qt, g = divmod(r, G)
                group = b * NG + (ph.base["qk"] + j)
                if r == 0:
                    for which in range(2):
                        pe.wait_ge(stacked[which], 16 * 3 * G * (group + 1))
                if n >= S_BANKS:
                    done = rowmin_done if ph.kind == "keys" else scores_read
                    pe.wait_ge(done, b * ITEMS + (ph.base["item"] + n - S_BANKS + 1))
                mm(score_bank[n % S_BANKS][:, :], q_stack[0:3 * HD, j % 2, g, qt * P:(qt + 1) * P],
                   k_stack[0:3 * HD, j % 2, g, :], start=True, stop=True).then_inc(scores_done, 1)

            def trans_bank_free(ph, b, e):
                if e >= T_BANKS:
                    pe.wait_ge(trans_read, b * (ITEMS + NG) + (ph.base["tentry"] + e - T_BANKS + 1))

            def transpose_item(ph, b, n):
                e = t_entry(n)
                pe.wait_ge(exp_done, b * ITEMS + (ph.base["item"] + n + 1))
                trans_bank_free(ph, b, e)
                for kt in range(KT):
                    last = nc.tensor.transpose(trans_bank[e % T_BANKS][:, kt * P:(kt + 1) * P],
                                               probs[:, n % U_RING, kt * P:(kt + 1) * P], ident[:, :])
                last.then_inc(trans_done, 1)

            def values(ph, b, step, rep, k):
                for kt in range(KT):
                    m = step - LAG_AV - kt
                    if not 0 <= m < ITEMS:
                        continue
                    j, r = divmod(m, TT * G)
                    qt, g = divmod(r, G)
                    if kt == 0:
                        if r == 0:
                            pe.wait_ge(job_freed, rep + (k + 3 * j + freed_dd(ph)))
                            if j >= 2:
                                pe.wait_ge(ctx_done, b * NG + (ph.base["group"] + j - 1))
                        pe.wait_ge(trans_read, b * (ITEMS + NG) + (ph.base["tentry"] + t_entry(m) + 1))
                    product = mm(av_bank[j % 2][HD * g:HD * (g + 1), qt * P:(qt + 1) * P],
                                 v_sb[:, j % 2, kt, HD * g:HD * (g + 1)], pT[:, m % PT_RING, kt, :],
                                 start=kt == 0, stop=kt == KT - 1)
                    if kt == KT - 1:
                        product.then_inc(av_done, 1)

            def reciprocals(ph, b, j):
                e = rb_entry(j)
                pe.wait_ge(rspread_done, b * NG + (ph.base["group"] + j + 1))
                trans_bank_free(ph, b, e)
                for qt in range(TT):
                    last = nc.tensor.transpose(trans_bank[e % T_BANKS][:, qt * P:(qt + 1) * P],
                                               rspread[:, qt * P:(qt + 1) * P], ident[:, :])
                last.then_inc(trans_done, 1)

            def out_job(ph, b, tt, rep, k):
                bank_free(ph, rep, k)
                t = slice(tt * P, (tt + 1) * P)
                for kt in range(KT):
                    last = three(job_bank_of(k)[:, :], (ctxT_hi[:, kt, t], ctxT_lo[:, kt, t]),
                                 (w_hi[:, 3, kt, :], w_lo[:, 3, kt, :]), kt == 0, kt == KT - 1)
                last.then_inc(job_done, 1)

            def attention_body(ph, b, to):
                rep, k = start(ph, b)
                dd = freed_dd(ph)
                kp = k + 3 * (NG - 1)
                group3 = ITEMS - TT * G
                for n in range(STEPS):
                    j, i = divmod(n, TT * G)
                    if n < ITEMS:
                        scores(ph, b, n)
                    if 0 <= n - LAG_T < ITEMS:
                        transpose_item(ph, b, n - LAG_T)
                    values(ph, b, n, rep, k)
                    for jj in range(NG):
                        if n == rb_step(jj):
                            reciprocals(ph, b, jj)
                    if j < NG - 1 and i < 3 * KT:
                        which, part = divmod(i, KT)
                        if part == 0:
                            bank_free(ph, rep, k + 3 * j + which)
                        project(ph, j + 1, which, k + 3 * j + which, [part])
                    for tile, at in zip(range(to[0].tiles), (2, 4, 6, 8, 9, 10, 13, 14)):
                        if n == group3 + at:
                            bank_free(ph, rep, kp + tile)
                            prologue_tile(*to, tile, kp + tile)
                    for which in range(3):
                        if to[0].attention and n == ITEMS + 2 * which:
                            kq = kp + to[0].tiles + which
                            if which == 0:
                                y_ready(*to)
                            if which == 1:
                                pe.wait_ge(job_freed, rep + (kp + to[0].tiles + dd))
                            if to[0] is not ph:
                                weights_ready(to[0], which)
                            bank_free(ph, rep, kq)
                            project(to[0], 0, which, kq)
                ko = out_place(k, to)
                weights_ready(ph, 3)
                pe.wait_ge(ctx_lo_done, b * NG + (ph.base["group"] + NG))
                for tt in range(TT):
                    out_job(ph, b, tt, rep, ko + tt)

            def mlp_body(ph, b, to):
                rep, k = start(ph, b)
                order = mlp_order(to)
                y_ready(ph, b)
                for l, (kind, n) in enumerate(order):
                    by_act, freed = mlp_freed(ph, b, order, l - 2)
                    pe.wait_ge(job_freed_act if by_act else job_freed, freed)
                    if kind == "up":
                        if n % KT == 0:
                            weights_ready(ph, n // KT)
                        c = slice((n % KT) * P, (n % KT + 1) * P)
                        for kt in range(KT):
                            end = three(job_bank_of(k + l)[:, :], (w_hi[:, n // KT, kt, c], w_lo[:, n // KT, kt, c]),
                                        (yT_hi[:, kt, :], yT_lo[:, kt, :]), kt == 0, kt == KT - 1)
                        end.then_inc(job_done, 1)
                    elif kind == "tile":
                        prologue_tile(*to, n, k + l)
                    elif kind == "down":
                        if n == 0:
                            weights_ready(ph, 3)
                            pe.wait_ge(h_lo_done, b * UP + (ph.base["h"] + UP))
                        t = slice(n * P, (n + 1) * P)
                        for m in range(UP):
                            end = three(job_bank_of(k + l)[:, :], (hT_hi[:, m, t], hT_lo[:, m, t]),
                                        (w_hi[:, 2 + m // KT, m % KT, :], w_lo[:, 2 + m // KT, m % KT, :]),
                                        m == 0, m == UP - 1)
                        end.then_inc(job_done, 1)
                    else:
                        if n == 0:
                            y_ready(*to)
                        if n == 1:
                            pe.wait_ge(job_freed, mlp_freed(ph, b, order, order.index(("tile", to[0].tiles - 1)))[1])
                        weights_ready(to[0], n)
                        project(to[0], 0, n, k + l)

            pe.wait_ge(const_done, 3)
            pe.wait_ge(vec_loaded, 16 * len(vec_names))
            nc.tensor.transpose(av_bank[0][:, 0:vec_cols], vec_rows, ident[0:vec_cols, 0:vec_cols]).then_inc(vec_turned, 1)
            first = phases[0]
            for tile in range(first.tiles):
                bank_free(first, 0, tile)
                prologue_tile(first, 0, tile, tile)
            y_ready(first, 0)
            for which in range(3):
                weights_ready(first, which)
                bank_free(first, 0, first.tiles + which)
                project(first, 0, which, first.tiles + which)
            for ph in phases:
                bodies(pe, ph, attention_body if ph.attention else mlp_body)

        @block.vector
        def _(dve):
            def ln_moments(ph, b, t):
                s = t % 2
                n = b * TT + (ph.base["tile_ln"] + t + 1)
                dve.wait_ge(x_loaded[s], 16 * (b * (ph.tiles // 2) + (ph.base[f"x{s}"] + t // 2 + 1)))
                nc.vector.bn_stats(stats[:, s, :], xin[:, s, :]).then_inc(ln_stats, 1)
                dve.wait_ge(ln_stats, n)
                alone(dve, dve_held)
                nc.vector.bn_aggr(moments[:, s, :], stats[:, s, :]).then_inc(ln_mom, 1)

            def ln_normalise(ph, b, t):
                s = t % 2
                dve.wait_ge(ln_rstd, b * TT + (ph.base["tile_ln"] + t + 1))
                nc.vector.tensor_scalar(xin[:, s, :], xin[:, s, :], moments[:, s, 0:1], rstd[:, s, 1:2],
                                        ALU.subtract, ALU.mult).then_inc(ln_norm, 1)

            def ln_scale(ph, b, t, done, bank_, y32):
                dve.wait_ge(job_done, done)
                if t >= 2:
                    dve.wait_ge(y_lo_done, b * TT + (ph.base["tile_ln"] + t - 1))
                for ft in range(KT):
                    op = nc.vector.tensor_scalar(y32[:, t % 2, ft, :], bank_[:, ft * P:(ft + 1) * P],
                                                 vec(ph.ln[0], ft), vec(ph.ln[1], ft), ALU.mult, ALU.add)
                op.then_inc(job_freed, 1)

            def enc_low(ph, b, t, k):
                dve.wait_ge(enc_hi_done, b * TT + (ph.base["enc"] + t + 1))
                ts = slice(t * P, (t + 1) * P)
                nc.vector.tensor_tensor(encT_lo[:, :, ts], job_bank_of(k)[:, :].rearrange("p (k q) -> p k q", q=P),
                                        encT_hi[:, :, ts].bitcast(f32), ALU.subtract).then_inc(job_freed, 1)

            def qk_low(ph, b, j, which, k):
                name, c = (ph.bq, ph.bk)[which]
                dve.wait_ge(qk_hi_done, 2 * (b * NG + (ph.base["qk"] + j)) + (which + 1))
                nc.vector.scalar_tensor_tensor(out=qk_lo[:, which, :], in0=job_bank_of(k)[:, :], scalar=vec(name, c + j),
                                               in1=qk_hi[:, which, :].bitcast(f32), op0=ALU.add, op1=ALU.subtract)\
                    .then_inc(job_freed, 1)

            def v_copy(ph, b, j, rep, k):
                dve.wait_ge(job_done, rep + (k + 1))
                if j >= 2:
                    dve.wait_ge(av_done, b * ITEMS + (ph.base["item"] + TT * G * (j - 1)))
                nc.vector.tensor_copy(v_sb[:, j % 2, :, :], job_bank_of(k)[:, :].rearrange("p (t f) -> p t f", f=P))\
                    .then_inc(job_freed, 1)

            def front(ph, b, n):
                item = b * ITEMS + ph.base["item"]
                m_done = ph.base["mask"]
                qt = n // G % TT
                if ph.kind == "keys":
                    if n >= ITEMS:
                        return
                    dve.wait_ge(scores_done, item + (n + 1))
                    if n >= U_RING:
                        dve.wait_ge(trans_done, b * (ITEMS + NG) + (ph.base["tentry"] + t_entry(n - U_RING) + 1))
                    if n == 0:
                        dve.wait_ge(w_lo_done, ph.base["weight"] + PIECES)
                        dve.wait_ge(mask_done, b + (m_done + 1))
                    alone(dve, dve_held)
                    nc.vector.tensor_tensor_reduce(out=probs[:, n % U_RING, :], in0=score_bank[n % S_BANKS][:, :],
                                                   in1=maskadd[:, 0, :], scale=-SCALE, scalar=3.0e38, op0=ALU.add,
                                                   op1=ALU.min, accum_out=rowmin[:, n:n + 1]).then_inc(rowmin_done, 1)
                    return
                if n < ITEMS:
                    dve.wait_ge(scores_done, item + (n + 1))
                    if n >= U_RING:
                        dve.wait_ge(trans_done, b * (ITEMS + NG) + (ph.base["tentry"] + t_entry(n - U_RING) + 1))
                    if n == 0:
                        dve.wait_ge(w_lo_done, ph.base["weight"] + PIECES)
                        dve.wait_ge(mask_done, m_done + TT if ph.kind == "self" else b * TT + (m_done + TT))
                    if n >= 1:
                        dve.wait_ge(scores_read, item + n)
                    nc.vector.scalar_tensor_tensor(out=probs[:, n % U_RING, :], in0=score_bank[n % S_BANKS][:, :],
                                                   scalar=-SCALE, in1=mask[:, qt, :], op0=ALU.mult, op1=ALU.mult)\
                        .then_inc(scores_read, 1)
                if 1 <= n <= ITEMS:
                    m = n - 1
                    if n == ITEMS:
                        dve.wait_ge(scores_read, item + ITEMS)
                        alone(dve, dve_held)
                    nc.vector.tensor_tensor_reduce(out=probs[:, m % U_RING, :], in0=probs[:, m % U_RING, :],
                                                   in1=maskadd[:, m // G % TT, :], scale=1.0, scalar=3.0e38,
                                                   op0=ALU.add, op1=ALU.min, accum_out=rowmin[:, m:m + 1])\
                        .then_inc(rowmin_done, 1)

            def invert(ph, b, j):
                dve.wait_ge(exp_done, b * ITEMS + (ph.base["item"] + (j + 1) * TT * G))
                if j >= 1:
                    dve.wait_ge(rspread_done, b * NG + (ph.base["group"] + j))
                nc.vector.reciprocal(rinv[:, :], rowsum[:, j * TT * G:(j + 1) * TT * G]).then_inc(rinv_done, 1)

            def normalise(ph, b, j):
                dve.wait_ge(trans_read, b * (ITEMS + NG) + (ph.base["tentry"] + rb_entry(j) + 1))
                dve.wait_ge(av_done, b * ITEMS + (ph.base["item"] + TT * G * (j + 1)))
                nc.vector.tensor_tensor(ctx32[:, :], av_bank[j % 2][:, :], ctx32[:, :], ALU.mult).then_inc(ctx_done, 1)

            def ctx_low(ph, b, j):
                name, c = ph.bv
                dve.wait_ge(ctx_hi_done, b * NG + (ph.base["group"] + j + 1))
                nc.vector.scalar_tensor_tensor(out=ctxT_lo[:, j, :], in0=ctx32[:, :], scalar=vec(name, c + j),
                                               in1=ctxT_hi[:, j, :].bitcast(f32), op0=ALU.add, op1=ALU.subtract)\
                    .then_inc(ctx_lo_done, 1)

            def add_residual(ph, b, tt, done, k):
                s = tt % 2
                dve.wait_ge(job_done, done)
                if ph.out_bias:
                    dve.wait_ge(res_biased, b * TT + (ph.base["bias"] * B * TT + tt + 1))
                else:
                    dve.wait_ge(res_loaded[s], 16 * (b * (TT // 2) + (ph.base[f"res{s}"] + tt // 2 + 1)))
                nc.vector.tensor_tensor(res[:, s, :], job_bank_of(k)[:, :], res[:, s, :], ALU.add).then_inc(job_freed, 1)

            def mask_part(to, qt):
                dve.wait_ge(mask_loaded[qt], 16 * (to[1] + (to[0].base["mask"] // TT + 1)))
                nc.vector.tensor_scalar(maskadd[:, qt, :], mask[:, qt, :], 1.0, -10000.0, ALU.subtract, ALU.mult)\
                    .then_inc(mask_done, 1)

            def keys_part(to):
                dve.wait_ge(mask_loaded[TT - 1], 16 * (to[1] + (to[0].base["mask"] // TT + 1)))
                nc.vector.tensor_scalar(maskadd[:, 0, :], mask_u8, 1.0, MASKED, ALU.subtract, ALU.mult)\
                    .then_inc(mask_done, 1)

            def hidden_low(ph, b, m):
                dve.wait_ge(h_hi_done, b * UP + (ph.base["h"] + m + 1))
                nc.vector.tensor_tensor(hT_lo[:, m, :], h32[:, m % 3, :, :].rearrange("p k q -> p (k q)"),
                                        hT_hi[:, m, :].bitcast(f32), ALU.subtract).then_inc(h_lo_done, 1)

            def attention_body(ph, b, to):
                rep, k = start(ph, b)
                kp = k + 3 * (NG - 1)
                group3 = ITEMS - TT * G
                for n in range(STEPS):
                    j, i = divmod(n, TT * G)
                    front(ph, b, n)
                    if j < NG - 1:
                        if i == 5:
                            qk_low(ph, b, j + 1, 0, k + 3 * j)
                        if i == 9:
                            qk_low(ph, b, j + 1, 1, k + 3 * j + 1)
                        if i == 13:
                            v_copy(ph, b, j + 1, rep, k + 3 * j + 2)
                    for jj in range(NG):
                        if n == rb_step(jj) - 2:
                            invert(ph, b, jj)
                        if n == norm_step(jj):
                            normalise(ph, b, jj)
                        if n == norm_step(jj) + 1:
                            ctx_low(ph, b, jj)
                    for t in range(TT):
                        if n == group3 + 2 * t:
                            ln_moments(*to, t)
                        if n == group3 + 2 * t + 1:
                            ln_normalise(*to, t)
                        if n == group3 + 2 * t + 3:
                            ln_scale(*to, t, rep + (kp + t + 1), job_bank_of(kp + t), y32_of[True])
                        if to[0].cross and n == group3 + (10, 11, 14, 15)[t]:
                            enc_low(*to, t, kp + TT + t)
                        if to[0].kind == "cross" and n == group3 + G * t + 9:
                            dve.wait_ge(rowmin_done, b * ITEMS + (ph.base["item"] + group3 + G * (t + 1)))
                            mask_part(to, t)
                    if to[0].kind == "keys" and n == ITEMS:
                        dve.wait_ge(rowmin_done, b * ITEMS + (ph.base["item"] + ITEMS))
                        keys_part(to)
                    if to[0].attention:
                        if n == ITEMS + 2:
                            qk_low(*to, 0, 0, kp + to[0].tiles)
                        if n == ITEMS + 4:
                            qk_low(*to, 0, 1, kp + to[0].tiles + 1)
                        if n == ITEMS + 6:
                            v_copy(*to, 0, rep, kp + to[0].tiles + 2)
                ko = out_place(k, to)
                for tt in range(TT):
                    add_residual(ph, b, tt, rep + (ko + tt + 1), ko + tt)

            def mlp_body(ph, b, to):
                rep, k = start(ph, b)
                order = mlp_order(to)

                def place(job):
                    return k + order.index(job)

                def down(tt):
                    kk = place(("down", tt))
                    add_residual(ph, b, tt, rep + (kk + 1), kk)

                if to:
                    for t in range(2):
                        ln_moments(*to, t)
                        ln_normalise(*to, t)
                    if to[0].kind == "keys":
                        keys_part(to)
                for m in range(UP):
                    hidden_low(ph, b, m)
                for half in range(2):
                    pair = (2 * half, 2 * half + 1)
                    if to:
                        for t in pair:
                            kk = place(("tile", t))
                            ln_scale(*to, t, rep + (kk + 1), job_bank_of(kk), y32_of[False])
                        if half == 0:
                            for t in (2, 3):
                                ln_moments(*to, t)
                                ln_normalise(*to, t)
                    for tt in pair:
                        down(tt)
                if to and to[0].cross:
                    for t in range(TT):
                        enc_low(*to, t, place(("tile", TT + t)))
                    for which in range(2):
                        qk_low(*to, 0, which, place(("qkv", which)))
                    v_copy(*to, 0, rep, place(("qkv", 2)))

            dve.wait_ge(vec_turned, 1)
            nc.vector.tensor_copy(vecs[:, :], av_bank[0][:, 0:vec_cols]).then_inc(vec_done, 1)
            dve.wait_ge(vec_done, 1)
            first = phases[0]
            for t in range(TT):
                ln_moments(first, 0, t)
                ln_normalise(first, 0, t)
                ln_scale(first, 0, t, t + 1, job_bank_of(t), y32_of[True])
            for qt in range(TT):
                mask_part((first, 0), qt)
            for which in range(2):
                qk_low(first, 0, 0, which, first.tiles + which)
            v_copy(first, 0, 0, 0, first.tiles + 2)
            for ph in phases:
                bodies(dve, ph, attention_body if ph.attention else mlp_body)

        @block.scalar
        def _(act):
            def y_high(ph, b, t, freed, y32):
                act.wait_ge(job_freed, freed)
                nc.scalar.activation(yT_hi[:, :, t * P:(t + 1) * P], y32[:, t % 2, :, :], ACT.Copy).then_inc(y_hi_done, 1)

            def enc_high(ph, b, t, rep, k):
                act.wait_ge(job_done, rep + (k + 1))
                nc.scalar.activation(encT_hi[:, :, t * P:(t + 1) * P],
                                     job_bank_of(k)[:, :].rearrange("p (k q) -> p k q", q=P), ACT.Copy)\
                    .then_inc(enc_hi_done, 1)

            def qk_high(ph, b, j, which, rep, k):
                name, c = (ph.bq, ph.bk)[which]
                act.wait_ge(job_done, rep + (k + 1))
                ge(act, stacked[which], 16 * 3 * G * (b * NG + (ph.base["qk"] + j)))
                nc.scalar.activation(qk_hi[:, which, :], job_bank_of(k)[:, :], ACT.Identity, bias=vec(name, c + j))\
                    .then_inc(qk_hi_done, 1)

            def exponent(ph, b, n):
                act.wait_ge(rowmin_done, b * ITEMS + (ph.base["item"] + n + 1))
                nc.scalar.activation(probs[:, n % U_RING, :], probs[:, n % U_RING, :], ACT.Exp, bias=rowmin[:, n:n + 1],
                                     scale=-1.0, accum_out=rowsum[:, n:n + 1]).then_inc(exp_done, 1)

            def copy_item(ph, b, n):
                e = t_entry(n)
                act.wait_ge(trans_done, b * (ITEMS + NG) + (ph.base["tentry"] + e + 1))
                if n >= PT_RING:
                    act.wait_ge(av_done, b * ITEMS + (ph.base["item"] + n - PT_RING + 1))
                nc.scalar.activation(pT[:, n % PT_RING, :, :].rearrange("p k q -> p (k q)"), trans_bank[e % T_BANKS][:, :],
                                     ACT.Copy).then_inc(trans_read, 1)

            def copy_reciprocals(ph, b, j):
                e = rb_entry(j)
                act.wait_ge(trans_done, b * (ITEMS + NG) + (ph.base["tentry"] + e + 1))
                if j >= 1:
                    act.wait_ge(ctx_lo_done, b * NG + (ph.base["group"] + j))
                nc.scalar.activation(ctx32[:, :], trans_bank[e % T_BANKS][:, :], ACT.Copy).then_inc(trans_read, 1)

            def ctx_high(ph, b, j):
                name, c = ph.bv
                act.wait_ge(ctx_done, b * NG + (ph.base["group"] + j + 1))
                nc.scalar.activation(ctxT_hi[:, j, :], ctx32[:, :], ACT.Identity, bias=vec(name, c + j))\
                    .then_inc(ctx_hi_done, 1)

            def weight_fetch(ph, piece):
                slot, kt = divmod(piece, KT)
                if piece >= RAW:
                    act.wait_ge(w_lo_done, ph.base["weight"] + piece - RAW + 1)
                act.dma_start(raw_of(ph, piece), ph.weights[slot](kt)).then_inc(w_loaded[piece % RAW], 16)

            def weight_high(ph, piece, upto):
                slot, kt = divmod(piece, KT)
                if piece + RAW - 1 < upto:
                    weight_fetch(ph, piece + RAW - 1)
                act.wait_ge(w_loaded[piece % RAW], 16 * ((ph.base["weight"] + piece) // RAW + 1))
                nc.scalar.activation(w_hi[:, slot, kt, :], raw_of(ph, piece), ACT.Copy).then_inc(w_hi_done, 1)

            def weight_run(ph, first, upto):
                for piece in range(first, min(first + RAW - 1, upto)):
                    weight_fetch(ph, piece)
                for piece in range(first, upto):
                    weight_high(ph, piece, upto)

            def attention_body(ph, b, to):
                rep, k = start(ph, b)
                kp = k + 3 * (NG - 1)
                dd = freed_dd(ph)
                group3 = ITEMS - TT * G
                fresh = to[0] is not ph
                for n in range(STEPS):
                    j, i = divmod(n, TT * G)
                    m = n - LAG_T - 1
                    if 0 <= m < ITEMS:
                        copy_item(ph, b, m)
                    if 1 <= n <= ITEMS:
                        exponent(ph, b, n - 1)
                    for jj in range(NG):
                        if n == rb_step(jj) + 1:
                            copy_reciprocals(ph, b, jj)
                        if n == norm_step(jj):
                            ctx_high(ph, b, jj)
                    if fresh and n == PREFETCH:
                        act.wait_ge(job_done, rep + kp)
                        for which in range(2):
                            act.wait_ge(stacked[which], 16 * 3 * G * (ph.base["qk"] + B * NG))
                        for piece in range(RAW - 1):
                            weight_fetch(to[0], piece)
                    if fresh and 0 <= n - PREFETCH < 3 * KT:
                        weight_high(to[0], n - PREFETCH, 3 * KT)
                    for which in range(2):
                        if j < NG - 1 and i == 4 + 4 * which:
                            qk_high(ph, b, j + 1, which, rep, k + 3 * j + which)
                        if to[0].attention and n == ITEMS + 1 + 2 * which:
                            if fresh:
                                act.wait_ge(w_lo_done, to[0].base["weight"] + 3 * KT)
                            qk_high(*to, 0, which, rep, kp + to[0].tiles + which)
                    for t in range(TT):
                        if n == group3 + 2 * t + 3:
                            y_high(*to, t, rep + (kp + t + 1 + dd), y32_of[True])
                        if to[0].cross and n == group3 + (9, 10, 13, 14)[t]:
                            enc_high(*to, t, rep, kp + TT + t)
                if fresh:
                    act.wait_ge(job_done, rep + (out_place(k, to) + TT))
                    weight_run(to[0], 3 * KT, PIECES)

            def mlp_body(ph, b, to):
                rep, k = start(ph, b)
                order = mlp_order(to)
                fresh = to and to[0] is not ph

                def hidden_high(m):
                    act.wait_ge(job_freed_act, b * UP + (ph.base["afree"] + m + 1))
                    nc.scalar.activation(hT_hi[:, m, :], h32[:, m % 3, :, :].rearrange("p k q -> p (k q)"), ACT.Copy)\
                        .then_inc(h_hi_done, 1)

                for m in range(UP):
                    act.wait_ge(job_done, rep + (k + m + 1))
                    if m >= 3:
                        act.wait_ge(h_lo_done, b * UP + (ph.base["h"] + m - 2))
                    nc.scalar.activation(h32[:, m % 3, :, :].rearrange("p k q -> p (k q)"), job_bank_of(k + m)[:, :],
                                         ACT.Gelu_apprx_tanh, bias=vec(ph.b1, ph.half * UP + m)).then_inc(job_freed_act, 1)
                    if m >= 1:
                        hidden_high(m - 1)
                hidden_high(UP - 1)
                for half in range(2):
                    if fresh:
                        weight_run(to[0], half * KT, (half + 1) * KT)
                    if to:
                        for t in (2 * half, 2 * half + 1):
                            y_high(*to, t, mlp_freed(ph, b, order, order.index(("tile", t)))[1], y32_of[False])
                if fresh:
                    if to[0].cross:
                        for t in range(TT):
                            enc_high(*to, t, rep, k + order.index(("tile", TT + t)))
                    act.wait_ge(job_done, rep + (k + order.index(("down", 3)) + 1))
                    weight_run(to[0], 2 * KT, 3 * KT)
                    if to[0].attention:
                        for which in range(2):
                            qk_high(*to, 0, which, rep, k + order.index(("qkv", which)))
                    weight_run(to[0], 3 * KT, PIECES)

            first = phases[0]
            weight_run(first, 0, KT)
            act.wait_ge(vec_done, 1)
            for t in range(TT):
                y_high(first, 0, t, t + 1, y32_of[True])
                weight_run(first, (t + 1) * KT, min((t + 2) * KT, PIECES))
            for which in range(2):
                qk_high(first, 0, 0, which, 0, first.tiles + which)
            for ph in phases:
                bodies(act, ph, attention_body if ph.attention else mlp_body)


_INS = ['x', 'ctx_2048', 'mask_1x1xSxS2_fc1', 'mask_Bx1xSxS2_ff1', 'mask_BxS2_bf1',
        'L0_xattn_ln1_s', 'L0_xattn_ln1_b', 'L0_xattn_w_qkv', 'L0_xattn_b_qkv', 'L0_xattn_w_ao', 'L0_xattn_b_ao',
        'L0_xattn_ln2_s', 'L0_xattn_ln2_b', 'L0_xattn_w_q', 'L0_xattn_b_q', 'L0_xattn_w_kv', 'L0_xattn_b_kv',
        'L0_xattn_w_co', 'L0_xattn_b_co', 'L0_xattn_ln3_s', 'L0_xattn_ln3_b', 'L0_xattn_w1', 'L0_xattn_b1',
        'L0_xattn_w2', 'L0_xattn_b2', 'L1_xattn_ln1_w', 'L1_xattn_ln1_b', 'L1_xattn_q_w', 'L1_xattn_q_b',
        'L1_xattn_k_w', 'L1_xattn_k_b', 'L1_xattn_v_w', 'L1_xattn_v_b', 'L1_xattn_cproj_w', 'L1_xattn_cproj_b',
        'L1_xattn_ln2_w', 'L1_xattn_ln2_b', 'L1_xattn_fc_w', 'L1_xattn_fc_b', 'L1_xattn_proj_w', 'L1_xattn_proj_b']


def kernel(**inputs):
    import numpy as _np
    import concourse.bacc as _bacc
    from concourse import mybir as _mybir
    from concourse.bass_utils import run_bass_kernel_spmd as _run

    nc = _bacc.Bacc("TRN2", target_bir_lowering=False, num_devices=1)
    arrays, aps = {}, {}
    for name in _INS:
        a = _np.ascontiguousarray(inputs[name])
        arrays[f"in_{name}"] = a
        aps[name] = nc.dram_tensor(f"in_{name}", a.shape, _mybir.dt.from_np(a.dtype), kind="ExternalInput").ap()
    out = nc.dram_tensor("out_0", (B, S, D), _mybir.dt.float32, kind="ExternalOutput").ap()
    xattn_program(nc, aps, out)
    r = _run(nc, [arrays], core_ids=[0])
    return r.results[0]["out_0"]
```

```python
import concourse.bass as bass
from concourse import mybir
from contextlib import ExitStack

P = 128
B, S, D = 4, 512, 512
HEADS, HD = 16, 32
HID = 4 * D
KT = D // P
TT = S // P
G = P // HD
NG = HEADS // G
EPS = 1e-5
SCALE = HD ** -0.5
MASKED = 1.7014118346046923e38

ITEMS = NG * TT * G
S_BANKS, T_BANKS, U_RING, PT_RING = 2, 2, 4, 5
LAG_T = 3
LAG_AV = LAG_T + 2
LAG_NORM = LAG_AV + KT + 1
STEPS = ITEMS + LAG_NORM + 1
UP = HID // 2 // P
SLOTS = 4
RAW = 4
PIECES = SLOTS * KT
PREFETCH = (NG - 1) * TT * G - 4
OUT_AT = [4 + part * 10 // 16 for part in range(TT * KT)]
LN_AT = [33, 36, 41, 44]
TILE_AT = [at + 3 for at in LN_AT] + [48, 50, 52, 54]
LOAD_AT = [24, 24] + [TILE_AT[t - 2] + 1 for t in range(2, 2 * TT)]
V_AT = [ITEMS + at for at in (2, 4, 9, 10)]


def qk_at(j, which):
    if j == 1:
        return [2 * which + part // 2 for part in range(KT)]
    first = {2: 14, 3: 26, NG: ITEMS - 7}[j]
    return [first + KT * which + part for part in range(KT)]


def ge(engine, sem, value):
    if isinstance(value, int) and value <= 0:
        return
    engine.wait_ge(sem, value)


def alone(engine, held):
    engine.sem_inc(held, 1)


class Phase:
    pass


class Counts:

    def __init__(self):
        self.at = {}

    def __getitem__(self, name):
        return self.at.get(name, 0)

    def add(self, name, n):
        self.at[name] = self[name] + n


def xattn_program(nc, ins, out):
    f32, f32r, u8 = mybir.dt.float32, mybir.dt.float32r, mybir.dt.uint8
    ACT = mybir.ActivationFunctionType
    ALU = mybir.AluOpType

    x_in = ins["x"].rearrange("b s d -> (b s) d")
    ctx_in = ins["ctx_2048"].rearrange("b s d -> (b s) d")
    out_rows = out.rearrange("b s d -> (b s) d")
    mask_shared = ins["mask_1x1xSxS2_fc1"].rearrange("a b q k -> (a b q) k")
    mask_batch = ins["mask_Bx1xSxS2_ff1"].rearrange("b a q k -> (b a q) k")
    mask_keys = ins["mask_BxS2_bf1"]
    resid = [nc.dram_tensor(f"resid{i}", (B * S, D), f32, kind="Internal").ap() for i in range(6)]

    L0, L1 = "L0_xattn_", "L1_xattn_"

    def cols(name, c):
        return lambda kt: ins[name][kt * P:(kt + 1) * P, c * D:(c + 1) * D]

    def rows(name, c):
        return lambda kt: ins[name][(c * KT + kt) * P:(c * KT + kt + 1) * P, :]

    phases = []

    def attention_phase(kind, src, dst, weights, ln, bq, bk, bv, bo):
        ph = Phase()
        ph.kind, ph.src, ph.dst, ph.weights = kind, src, dst, weights
        ph.ln, ph.bq, ph.bk, ph.bv, ph.out_bias = ln, bq, bk, bv, bo
        ph.attention, ph.cross = True, kind != "self"
        ph.tiles = 2 * TT if ph.cross else TT
        ph.pro_jobs = ph.tiles + 2 + TT
        ph.resid_src = src
        phases.append(ph)

    def mlp_phase(half, src, resid_src, dst, weights, ln, b1, b2):
        ph = Phase()
        ph.kind, ph.src, ph.resid_src, ph.dst, ph.weights = "mlp", src, resid_src, dst, weights
        ph.ln, ph.b1, ph.half, ph.out_bias = ln, b1, half, b2
        ph.attention, ph.cross = False, False
        ph.tiles = TT
        ph.pro_jobs = TT
        phases.append(ph)

    attention_phase("self", x_in, resid[0],
                    [cols(L0 + "w_qkv", 0), cols(L0 + "w_qkv", 1), cols(L0 + "w_qkv", 2), cols(L0 + "w_ao", 0)],
                    (L0 + "ln1_s", L0 + "ln1_b"), (L0 + "b_qkv", 0), (L0 + "b_qkv", 4), (L0 + "b_qkv", 8),
                    L0 + "b_ao")
    attention_phase("cross", resid[0], resid[1],
                    [cols(L0 + "w_q", 0), cols(L0 + "w_kv", 0), cols(L0 + "w_kv", 1), cols(L0 + "w_co", 0)],
                    (L0 + "ln2_s", L0 + "ln2_b"), (L0 + "b_q", 0), (L0 + "b_kv", 0), (L0 + "b_kv", 4),
                    L0 + "b_co")
    for h in range(2):
        mlp_phase(h, resid[1], resid[1 + h], resid[2 + h],
                  [cols(L0 + "w1", 2 * h), cols(L0 + "w1", 2 * h + 1), rows(L0 + "w2", 2 * h), rows(L0 + "w2", 2 * h + 1)],
                  (L0 + "ln3_s", L0 + "ln3_b"), L0 + "b1", None if h else L0 + "b2")
    attention_phase("keys", resid[3], resid[4],
                    [cols(L1 + "q_w", 0), cols(L1 + "k_w", 0), cols(L1 + "v_w", 0), cols(L1 + "cproj_w", 0)],
                    (L1 + "ln1_w", L1 + "ln1_b"), (L1 + "q_b", 0), (L1 + "k_b", 0), (L1 + "v_b", 0),
                    L1 + "cproj_b")
    for h in range(2):
        mlp_phase(h, resid[4], resid[4 + h], out_rows if h else resid[5],
                  [cols(L1 + "fc_w", 2 * h), cols(L1 + "fc_w", 2 * h + 1), rows(L1 + "proj_w", 2 * h), rows(L1 + "proj_w", 2 * h + 1)],
                  (L1 + "ln2_w", L1 + "ln2_b"), L1 + "fc_b", None if h else L1 + "proj_b")

    vec_at, vec_cols = {}, 0
    vec_names = []
    for ph in phases:
        names = list(ph.ln) + ([ph.bq[0], ph.bk[0], ph.bv[0]] if ph.attention else [ph.b1])
        for name in names:
            if name not in vec_at:
                vec_at[name] = vec_cols
                vec_names.append(name)
                vec_cols += ins[name].shape[0] // P

    counts = Counts()
    names = ("afree", "x0", "x1", "tile_ln", "item", "tentry", "group", "qk", "enc", "res0", "res1", "res2", "res3",
             "store0", "store1", "store2", "store3", "bias", "mask", "weight", "h")
    job, dfree = phases[0].pro_jobs, phases[0].pro_jobs
    for index, ph in enumerate(phases):
        ph.index = index
        ph.nxt = phases[index + 1] if index + 1 < len(phases) else None
        ph.base = {k: counts[k] for k in names}
        ph.job0, ph.dfree0 = job, dfree
        nxt_jobs = ph.nxt.pro_jobs if ph.nxt else 0
        if ph.attention:
            ph.jobs = 2 * (NG - 1) + ph.pro_jobs + TT
            ph.dfrees = ph.jobs
            counts.add("item", B * ITEMS)
            counts.add("tentry", B * (ITEMS + NG))
            counts.add("group", B * NG)
            counts.add("qk", B * NG)
            counts.add("enc", B * TT * ph.cross)
            counts.add("mask", {"self": TT, "cross": B * TT, "keys": B}[ph.kind])
        else:
            ph.jobs = UP + TT + TT
            ph.dfrees = 2 * TT
            counts.add("afree", B * UP)
            counts.add("h", B * UP)
        job += B * ph.jobs - ph.pro_jobs + nxt_jobs
        dfree += B * ph.dfrees - ph.pro_jobs + nxt_jobs
        counts.add("tile_ln", B * TT)
        for s in range(2):
            counts.add(f"x{s}", B * ph.tiles // 2)
        ph.res_slots = TT if ph.attention else 2
        for s in range(ph.res_slots):
            counts.add(f"res{s}", B * TT // ph.res_slots)
            counts.add(f"store{s}", B * TT // ph.res_slots)
        if ph.out_bias:
            counts.add("bias", 1)
        counts.add("weight", PIECES)

    ctx = ExitStack()
    with ctx:
        def sb(name, shape, dt=f32):
            return ctx.enter_context(nc.sbuf_tensor(name, shape, dt))

        def sem(name):
            return ctx.enter_context(nc.semaphore(name))

        w_hi = sb("w_hi", [P, SLOTS, KT, D], f32r)
        w_lo = sb("w_lo", [P, SLOTS, KT, D], f32r)
        xin = sb("xin", [P, 2, D])
        yT_hi = sb("yT_hi", [P, KT, S], f32r)
        yT_lo = sb("yT_lo", [P, KT, S], f32r)
        encT_hi = sb("encT_hi", [P, KT, S], f32r)
        encT_lo = sb("encT_lo", [P, KT, S], f32r)
        q_stack = sb("q_stack", [P, 2, G, S], f32r)
        k_stack = sb("k_stack", [P, 2, G, S], f32r)
        hT_hi = q_stack[:, :, :, :].rearrange("p a g s -> p (a g) s")
        hT_lo = k_stack[:, :, :, :].rearrange("p a g s -> p (a g) s")
        qk_parts = sb("qk_parts", [P, 2, 2, S])
        qk_hi, qk_lo = qk_parts[:, 0, :, :].bitcast(f32r), qk_parts[:, 1, :, :].bitcast(f32r)
        v_sb = sb("v_sb", [P, TT, D])
        probs = sb("probs", [P, U_RING, S])
        w_raw = probs
        w_raw_qk = qk_parts[:, :, :, :].rearrange("p a b s -> p (a b) s")
        pT = sb("pT", [P, PT_RING, KT, P])
        h32 = pT
        ctx32 = sb("ctx32", [P, S])
        rspread = ctx32
        vec_rows = rspread[0:vec_cols, 0:P]
        ctxT_hi = sb("ctxT_hi", [P, KT, S], f32r)
        ctxT_lo = sb("ctxT_lo", [P, KT, S], f32r)
        mask = sb("mask", [P, TT, S])
        maskadd = sb("maskadd", [P, TT, S])
        mask_u8 = mask[:, TT - 1, 0:P].bitcast(u8)
        res = sb("res", [P, 2, D])
        y32_of = {True: res[:, :, :].rearrange("p s (k q) -> p s k q", q=P),
                  False: mask[:, 0:2, :].rearrange("p s (k q) -> p s k q", q=P)}
        obias = sb("obias", [P, D])
        vecs = sb("vecs", [P, vec_cols])
        ident = sb("ident", [P, P])
        stats = sb("stats", [P, 2, 6])
        moments = sb("moments", [P, 2, 2])
        rstd = sb("rstd", [P, 2, 2])
        minus_half = sb("minus_half", [P, 1])
        rowmin = sb("rowmin", [P, ITEMS])
        rowsum = sb("rowsum", [P, ITEMS])
        rinv = sb("rinv", [P, TT * G])

        bank = [ctx.enter_context(nc.psum_tensor(f"bank{i}", [P, 512], f32)) for i in range(8)]
        score_bank, trans_bank, av_bank, job_bank = bank[0:2], bank[2:4], bank[4:6], bank[6:8]

        const_done = sem("const_done")
        vec_loaded = sem("vec_loaded")
        vec_turned = sem("vec_turned")
        vec_done = sem("vec_done")
        w_loaded = [sem(f"w_loaded{i}") for i in range(RAW)]
        w_hi_done = sem("w_hi_done")
        w_lo_done = sem("w_lo_done")
        bias_loaded = sem("bias_loaded")
        mask_loaded = [sem(f"mask_loaded{i}") for i in range(TT)]
        mask_done = sem("mask_done")
        x_loaded = [sem(f"x_loaded{i}") for i in range(2)]
        ln_stats = sem("ln_stats")
        ln_mom = sem("ln_mom")
        ln_eps = sem("ln_eps")
        ln_rstd = sem("ln_rstd")
        ln_norm = sem("ln_norm")
        y_hi_done = sem("y_hi_done")
        y_lo_done = sem("y_lo_done")
        enc_hi_done = sem("enc_hi_done")
        job_done = sem("job_done")
        job_freed = sem("job_freed")
        job_freed_act = sem("job_freed_act")
        qk_hi_done = sem("qk_hi_done")
        stacked = [sem("q_stacked"), sem("k_stacked")]
        scores_done = sem("scores_done")
        scores_read = sem("scores_read")
        rowmin_done = sem("rowmin_done")
        exp_done = sem("exp_done")
        trans_done = sem("trans_done")
        trans_read = sem("trans_read")
        av_done = sem("av_done")
        rinv_done = sem("rinv_done")
        rspread_done = sem("rspread_done")
        ctx_done = sem("ctx_done")
        ctx_hi_done = sem("ctx_hi_done")
        ctx_lo_done = sem("ctx_lo_done")
        h_hi_done = sem("h_hi_done")
        h_lo_done = sem("h_lo_done")
        res_loaded = [sem(f"res_loaded{i}") for i in range(TT)]
        res_biased = sem("res_biased")
        stored = [sem(f"stored{i}") for i in range(TT)]

        dve_held, pool_held, sp_held = sem("dve_held"), sem("pool_held"), sem("sp_held")

        block = ctx.enter_context(nc.Block())

        def dram_rows(t, b, tt):
            return t[bass.ds(b * S + tt * P, P), :]

        def vec(name, c):
            return vecs[:, vec_at[name] + c:vec_at[name] + c + 1]

        def t_entry(n):
            j = n // (TT * G)
            return n + sum(1 for jj in range(NG) if n > rb_item(jj))

        def rb_item(j):
            return min((j + 1) * TT * G - 1 + LAG_AV - LAG_T, ITEMS - 1)

        def rb_entry(j):
            return rb_item(j) + j + 1

        def rb_step(j):
            return (j + 1) * TT * G - 1 + LAG_AV

        def norm_step(j):
            return (j + 1) * TT * G - 1 + LAG_NORM

        def bodies(engine, ph, body):
            last = (ph.nxt, 0) if ph.nxt else None
            if ph.attention:
                body(ph, 0, (ph, 1), False)
                with engine.Fori(1, B - 1) as b:
                    body(ph, b, (ph, b + 1), True)
                body(ph, B - 1, last, True)
            else:
                body(ph, 0, (ph, 1), True)
                with engine.Fori(1, B - 1) as b:
                    body(ph, b, (ph, b + 1), False)
                body(ph, B - 1, last, False)

        def job_bank_of(k):
            return job_bank[k % 2]

        def start(ph, b, prev=False):
            return b * ph.jobs, ph.job0 - TT * prev

        def qk_place(k, prev, j, which):
            return k + 2 * (j - 1) + which + TT * (prev and j > 1)

        def pro_place(k, prev):
            return k + 2 * (NG - 1) + TT * prev

        def res_tile(ph, tt):
            return res[:, tt, :] if tt < 2 else xin[:, tt - 2, :] if ph.attention else res[:, tt - 2, :]

        def res_count(ph, b, tt, what, done):
            slots = ph.res_slots
            return 16 * (b * (TT // slots) + (ph.base[f"{what}{tt % slots}"] + tt // slots + done))

        def freed_dd(ph):
            return ph.dfree0 - ph.job0

        def out_place(k, to, prev):
            return pro_place(k, prev) + (to[0].pro_jobs if to else 0)

        def mlp_order(to):
            pro = [("tile", t) for t in range(to[0].tiles)] if to else []
            tail = [("qk", w) for w in range(2)] + [("v", t) for t in range(TT)] if to and to[0].attention else []
            return ([("up", m) for m in range(UP)] + pro[0:2] + [("down", 0), ("down", 1)] + pro[2:4]
                    + [("down", 2), ("down", 3)] + pro[4:] + tail)

        def mlp_freed(ph, b, order, l):
            d0 = b * ph.dfrees
            if l < 0:
                return False, d0 + (ph.dfree0 + l + 1)
            if order[l][0] == "up":
                return True, b * UP + (ph.base["afree"] + l + 1)
            return False, d0 + (ph.dfree0 + sum(1 for kind, _ in order[:l + 1] if kind != "up"))

        def mlp_bank(order, l):
            kind, n = order[l]
            return score_bank[n % 2] if kind == "tile" else job_bank[sum(kd != "tile" for kd, _ in order[:l]) % 2]

        def mlp_bank_before(order, l):
            same = [m for m in range(l) if mlp_bank(order, m) is mlp_bank(order, l)]
            if same:
                return same[-1]
            return -1 if order[l][0] == "tile" else l - 2

        def late_from(ph):
            if ph.attention:
                return PIECES
            return 3 * KT if phases[ph.index - 1].attention else 2 * KT

        def raw_of(ph, piece):
            shared = ph.index and phases[ph.index - 1].attention and piece < 3 * KT
            return (w_raw_qk if shared else w_raw)[:, piece % RAW, :]

        @block.sync
        def _(sp):
            def load_tile(to, tile, rep, before):
                ph, b = to
                if before is not None:
                    sp.wait_ge(job_done, rep + before)
                    alone(sp, sp_held)
                s = tile % 2
                src = ph.src if tile < TT else ctx_in
                sp.dma_start(xin[:, s, :], dram_rows(src, b, tile % TT)).then_inc(x_loaded[s], 16)

            def stack(ph, b, j, which, freed):
                st = (q_stack, k_stack)[which]
                sp.wait_ge(job_freed, freed)
                alone(sp, sp_held)
                places = ((0, qk_hi), (1, qk_lo), (2, qk_hi)) if which == 0 else ((0, qk_hi), (1, qk_hi), (2, qk_lo))
                for g in range(G):
                    for r, part in places:
                        sp.dma_start(st[HD * r:HD * (r + 1), j % 2, g, :].bitcast(f32),
                                     part[HD * g:HD * (g + 1), which, :].bitcast(f32)).then_inc(stacked[which], 16)

            def load_res(ph, b, tt):
                s = tt % ph.res_slots
                if tt >= ph.res_slots:
                    sp.wait_ge(stored[s], res_count(ph, b, tt, "store", 0))
                    alone(sp, sp_held)
                sp.dma_start(res_tile(ph, tt), dram_rows(ph.resid_src, b, tt)).then_inc(res_loaded[s], 16)

            def store(ph, b, tt, freed):
                sp.wait_ge(job_freed, freed)
                alone(sp, sp_held)
                sp.dma_start(dram_rows(ph.dst, b, tt), res_tile(ph, tt)).then_inc(stored[tt % ph.res_slots], 16)

            def all_stored(ph, b):
                for s in range(ph.res_slots):
                    sp.wait_ge(stored[s], res_count(ph, b, TT - ph.res_slots + s, "store", 1))
                    alone(sp, sp_held)

            def body_end(ph, b, to):
                all_stored(ph, b)
                if to and to[0] is not ph and to[0].out_bias:
                    sp.wait_ge(res_biased, to[0].base["bias"] * B * TT)
                    load_out_bias(to[0])

            def load_out_bias(ph):
                sp.dma_start(obias[:, :], ins[ph.out_bias].rearrange("(a n) -> a n", a=1).broadcast_to([P, D]))\
                    .then_inc(bias_loaded, 16)

            def load_mask(to, qt):
                sp.dma_start(mask[:, qt, :], dram_rows(mask_shared if to[0].kind == "self" else mask_batch, to[1], qt))\
                    .then_inc(mask_loaded[qt], 16)

            def load_keys(to):
                sp.dma_start(mask_u8, mask_keys[bass.ds(to[1], 1), :].broadcast_to([P, S])).then_inc(mask_loaded[TT - 1], 16)

            def attention_body(ph, b, to, prev):
                rep, k = start(ph, b, prev)
                dd = freed_dd(ph)
                kp = pro_place(k, prev)
                ko = out_place(k, to, prev)
                group3 = ITEMS - TT * G
                for n in range(STEPS):
                    for tt in range(TT):
                        if prev and n == OUT_AT[KT * tt + KT - 1] + 3:
                            store(ph, b - 1, tt, rep + (k + 2 + tt + 1 + dd))
                    if prev and n == LOAD_AT[0]:
                        all_stored(ph, b - 1)
                    for which in range(2):
                        for jj in range(1, NG):
                            if n == qk_at(jj, which)[-1] + 2:
                                if jj >= 2:
                                    sp.wait_ge(scores_done, b * ITEMS + (ph.base["item"] + TT * G * (jj - 1)))
                                    alone(sp, sp_held)
                                stack(ph, b, jj, which, rep + (qk_place(k, prev, jj, which) + 1 + dd))
                        if to[0].attention and n == qk_at(NG, which)[-1] + 2:
                            stack(*to, 0, which, rep + (kp + to[0].tiles + which + 1 + dd))
                    for tile in range(to[0].tiles):
                        if n == LOAD_AT[tile]:
                            load_tile(to, tile, rep, None if tile < 2 else kp + tile - 1)
                    for qt in range(TT):
                        if to[0].kind == "cross" and n == group3 + G * qt + 5:
                            sp.wait_ge(scores_read, b * ITEMS + (ph.base["item"] + group3 + G * (qt + 1)))
                            alone(sp, sp_held)
                            load_mask(to, qt)
                    if to[0].kind == "keys" and n == group3 + 5:
                        sp.wait_ge(mask_done, b + (ph.base["mask"] + 1))
                        alone(sp, sp_held)
                        load_keys(to)
                    if n == group3 + 12:
                        sp.wait_ge(y_lo_done, to[1] * TT + (to[0].base["tile_ln"] + TT))
                        alone(sp, sp_held)
                        sp.wait_ge(job_done, rep + (kp + to[0].tiles))
                        alone(sp, sp_held)
                        for tt in range(TT):
                            load_res(ph, b, tt)
                if to[0] is not ph:
                    for tt in range(TT):
                        store(ph, b, tt, rep + (ko + tt + 1 + dd))
                    body_end(ph, b, to)

            def mlp_body(ph, b, to, opens):
                rep, k = start(ph, b)
                order = mlp_order(to)

                def freed(job):
                    return mlp_freed(ph, b, order, order.index(job))[1]

                def tile(t):
                    load_tile(to, t, rep, None if t < 2 else k + order.index(("tile", t - 2)) + 1)

                sp.wait_ge(job_done, rep + (k + 1))
                alone(sp, sp_held)
                if to:
                    tile(0)
                    tile(1)
                    if to[0].kind == "keys":
                        load_keys(to)
                load_res(ph, b, 0)
                load_res(ph, b, 1)
                if to:
                    tile(2)
                    tile(3)
                store(ph, b, 0, freed(("down", 0)))
                load_res(ph, b, 2)
                store(ph, b, 1, freed(("down", 1)))
                load_res(ph, b, 3)
                if to and to[0].cross:
                    tile(4)
                    tile(5)
                store(ph, b, 2, freed(("down", 2)))
                store(ph, b, 3, freed(("down", 3)))
                if to and to[0].cross:
                    tile(6)
                    tile(7)
                    for which in range(2):
                        stack(*to, 0, which, freed(("qk", which)))
                body_end(ph, b, to)

            first = phases[0]
            load_tile((first, 0), 0, 0, None)
            load_tile((first, 0), 1, 0, None)
            for name in vec_names:
                n = ins[name].shape[0] // P
                sp.dma_start(vec_rows[vec_at[name]:vec_at[name] + n, :], ins[name].rearrange("(t p) -> t p", p=P))\
                    .then_inc(vec_loaded, 16)
            for tile_ in range(2, TT):
                load_tile((first, 0), tile_, 0, tile_ - 1)
            load_out_bias(first)
            for qt in range(TT):
                load_mask((first, 0), qt)
            for which in range(2):
                stack(first, 0, 0, which, first.tiles + which + 1)
            for ph in phases:
                bodies(sp, ph, attention_body if ph.attention else mlp_body)

        @block.gpsimd
        def _(pool):
            nc.gpsimd.memset(ident[:, :], 0.0).then_inc(const_done, 1)
            nc.gpsimd.memset(minus_half[:, :], -0.5).then_inc(const_done, 1)
            pool.wait_ge(const_done, 2)
            nc.gpsimd.affine_select(out=ident[:, :], in_=ident[:, :], compare_op=ALU.not_equal, fill=1.0, base=0,
                                    pattern=[[-1, P]], channel_multiplier=1).then_inc(const_done, 1)
            def weight_low(ph, piece):
                slot, kt = divmod(piece, KT)
                pool.wait_ge(w_hi_done, ph.base["weight"] + piece + 1)
                nc.gpsimd.tensor_tensor(w_lo[:, slot, kt, :], raw_of(ph, piece), w_hi[:, slot, kt, :].bitcast(f32),
                                        ALU.subtract).then_inc(w_lo_done, 1)

            def ln_power(ph, b, t):
                n = b * TT + (ph.base["tile_ln"] + t + 1)
                pool.wait_ge(ln_mom, n)
                alone(pool, pool_held)
                nc.gpsimd.tensor_scalar(rstd[:, t % 2, 0:1], moments[:, t % 2, 1:2], EPS, None, ALU.add).then_inc(ln_eps, 1)
                pool.wait_ge(ln_eps, n)
                nc.gpsimd.tensor_tensor(rstd[:, t % 2, 1:2], rstd[:, t % 2, 0:1], minus_half[:, :], ALU.pow).then_inc(ln_rstd, 1)

            def y_low(ph, b, t, y32):
                pool.wait_ge(y_hi_done, b * TT + (ph.base["tile_ln"] + t + 1))
                nc.gpsimd.tensor_tensor(yT_lo[:, :, t * P:(t + 1) * P], y32[:, t % 2, :, :],
                                        yT_hi[:, :, t * P:(t + 1) * P].bitcast(f32), ALU.subtract).then_inc(y_lo_done, 1)

            def spread(ph, b, j):
                group = b * NG + (ph.base["group"] + j)
                pool.wait_ge(rinv_done, group + 1)
                ge(pool, ctx_lo_done, group)
                if ph.index == 0 and j == 0:
                    pool.wait_ge(vec_turned, 1)
                alone(pool, pool_held)
                nc.gpsimd.tensor_copy(rspread[:, :].rearrange("p (n d) -> p n d", d=HD),
                                      rinv[:, :].unsqueeze(2).broadcast_to([P, TT * G, HD])).then_inc(rspread_done, 1)

            def bias_res(ph, b, tt):
                pool.wait_ge(res_loaded[tt % ph.res_slots], res_count(ph, b, tt, "res", 1))
                nc.gpsimd.tensor_tensor(res_tile(ph, tt), res_tile(ph, tt), obias[:, :], ALU.add).then_inc(res_biased, 1)

            def attention_body(ph, b, to, prev):
                for n in range(STEPS):
                    if prev and n < TT:
                        bias_res(ph, b - 1, n)
                    for t in range(TT):
                        if n == LN_AT[t]:
                            ln_power(*to, t)
                        if n == LN_AT[t] + 4:
                            y_low(*to, t, y32_of[True])
                    for j in range(NG):
                        if n == rb_step(j) - 1:
                            spread(ph, b, j)
                    if to[0] is not ph and 0 <= n - PREFETCH < 3 * KT:
                        weight_low(to[0], n - PREFETCH)
                if to[0] is not ph:
                    for tt in range(TT):
                        bias_res(ph, b, tt)
                    for piece in range(3 * KT, late_from(to[0])):
                        weight_low(to[0], piece)

            def mlp_body(ph, b, to, opens):
                fresh = to and to[0] is not ph
                if to:
                    ln_power(*to, 0)
                    ln_power(*to, 1)
                if opens:
                    for piece in range(late_from(ph), PIECES):
                        weight_low(ph, piece)
                if ph.out_bias:
                    bias_res(ph, b, 0)
                    bias_res(ph, b, 1)
                if to:
                    for t in range(2):
                        y_low(*to, t, y32_of[False])
                        ln_power(*to, t + 2)
                if fresh:
                    for piece in range(KT):
                        weight_low(to[0], piece)
                if to:
                    y_low(*to, 2, y32_of[False])
                    y_low(*to, 3, y32_of[False])
                if ph.out_bias:
                    bias_res(ph, b, 2)
                    bias_res(ph, b, 3)
                if fresh:
                    for piece in range(KT, 2 * KT):
                        weight_low(to[0], piece)
                if fresh:
                    for piece in range(2 * KT, late_from(to[0])):
                        weight_low(to[0], piece)

            first = phases[0]
            for piece in range(KT):
                weight_low(first, piece)
            ln_power(first, 0, 0)
            for t in range(TT):
                if t + 1 < TT:
                    ln_power(first, 0, t + 1)
                y_low(first, 0, t, y32_of[True])
                if t != 2:
                    slot = t + 1 if t < 2 else t
                    for piece in range(slot * KT, (slot + 1) * KT):
                        weight_low(first, piece)
            for ph in phases:
                if ph.out_bias:
                    pool.wait_ge(bias_loaded, 16 * (ph.base["bias"] + 1))
                bodies(pool, ph, attention_body if ph.attention else mlp_body)

        @block.tensor
        def _(pe):
            mm = nc.tensor.matmul

            def three(dst, lhs, rhs, first, last):
                mm(dst, lhs[0], rhs[0], start=first, stop=False)
                mm(dst, lhs[0], rhs[1], start=False, stop=False)
                return mm(dst, lhs[1], rhs[0], start=False, stop=last)

            def bank_free(ph, rep, k):
                ge(pe, job_freed, rep + (k - 1 + freed_dd(ph)))

            def transposes(dst, slot):
                for ft in range(KT):
                    ins_ = nc.tensor.transpose(dst[:, ft * P:(ft + 1) * P], xin[:, slot, ft * P:(ft + 1) * P],
                                               ident[:, :])
                ins_.then_inc(job_done, 1)

            def ln_job(ph, b, t, dst):
                pe.wait_ge(ln_norm, b * TT + (ph.base["tile_ln"] + t + 1))
                transposes(dst, t % 2)

            def enc_job(ph, b, t, dst):
                s = t % 2
                pe.wait_ge(x_loaded[s], 16 * (b * (ph.tiles // 2) + (ph.base[f"x{s}"] + TT // 2 + t // 2 + 1)))
                transposes(dst, s)

            def weights_ready(ph, slot):
                pe.wait_ge(w_lo_done, ph.base["weight"] + KT * (slot + 1))

            def y_ready(ph, b):
                pe.wait_ge(y_lo_done, b * TT + (ph.base["tile_ln"] + TT))

            def qk_part(ph, j, which, k, kt):
                hi, lo = (encT_hi, encT_lo) if which and ph.cross else (yT_hi, yT_lo)
                c = slice(j * P, (j + 1) * P)
                return three(job_bank_of(k)[:, :], (w_hi[:, which, kt, c], w_lo[:, which, kt, c]),
                             (hi[:, kt, :], lo[:, kt, :]), kt == 0, kt == KT - 1)

            def v_job(ph, tt, k):
                hi, lo = (encT_hi, encT_lo) if ph.cross else (yT_hi, yT_lo)
                t = slice(tt * P, (tt + 1) * P)
                for kt in range(KT):
                    last = three(job_bank_of(k)[:, :], (hi[:, kt, t], lo[:, kt, t]),
                                 (w_hi[:, 2, kt, :], w_lo[:, 2, kt, :]), kt == 0, kt == KT - 1)
                last.then_inc(job_done, 1)

            def qk_job(ph, j, which, k, parts=range(KT)):
                for kt in parts:
                    last = qk_part(ph, j, which, k, kt)
                    if kt == KT - 1:
                        last.then_inc(job_done, 1)

            def prologue_tile(ph, b, tile, dst):
                if tile < TT:
                    ln_job(ph, b, tile, dst)
                else:
                    enc_job(ph, b, tile - TT, dst)

            def scores(ph, b, n):
                j, r = divmod(n, TT * G)
                qt, g = divmod(r, G)
                group = b * NG + (ph.base["qk"] + j)
                if r == 0:
                    for which in range(2):
                        pe.wait_ge(stacked[which], 16 * 3 * G * (group + 1))
                if n >= S_BANKS:
                    done = rowmin_done if ph.kind == "keys" else scores_read
                    pe.wait_ge(done, b * ITEMS + (ph.base["item"] + n - S_BANKS + 1))
                mm(score_bank[n % S_BANKS][:, :], q_stack[0:3 * HD, j % 2, g, qt * P:(qt + 1) * P],
                   k_stack[0:3 * HD, j % 2, g, :], start=True, stop=True).then_inc(scores_done, 1)

            def trans_bank_free(ph, b, e):
                if e >= T_BANKS:
                    pe.wait_ge(trans_read, b * (ITEMS + NG) + (ph.base["tentry"] + e - T_BANKS + 1))

            def transpose_item(ph, b, n):
                e = t_entry(n)
                pe.wait_ge(exp_done, b * ITEMS + (ph.base["item"] + n + 1))
                trans_bank_free(ph, b, e)
                for kt in range(KT):
                    last = nc.tensor.transpose(trans_bank[e % T_BANKS][:, kt * P:(kt + 1) * P],
                                               probs[:, n % U_RING, kt * P:(kt + 1) * P], ident[:, :])
                last.then_inc(trans_done, 1)

            def values(ph, b, step, rep, k):
                for kt in range(KT):
                    m = step - LAG_AV - kt
                    if not 0 <= m < ITEMS:
                        continue
                    j, r = divmod(m, TT * G)
                    qt, g = divmod(r, G)
                    if kt == 0:
                        if m == 0:
                            pe.wait_ge(job_freed, rep + (k + freed_dd(ph)))
                        if r == 0 and j >= 2:
                            pe.wait_ge(ctx_done, b * NG + (ph.base["group"] + j - 1))
                        pe.wait_ge(trans_read, b * (ITEMS + NG) + (ph.base["tentry"] + t_entry(m) + 1))
                    product = mm(av_bank[j % 2][HD * g:HD * (g + 1), qt * P:(qt + 1) * P],
                                 v_sb[:, kt, j * P + HD * g:j * P + HD * (g + 1)], pT[:, m % PT_RING, kt, :],
                                 start=kt == 0, stop=kt == KT - 1)
                    if kt == KT - 1:
                        product.then_inc(av_done, 1)

            def reciprocals(ph, b, j):
                e = rb_entry(j)
                pe.wait_ge(rspread_done, b * NG + (ph.base["group"] + j + 1))
                trans_bank_free(ph, b, e)
                for qt in range(TT):
                    last = nc.tensor.transpose(trans_bank[e % T_BANKS][:, qt * P:(qt + 1) * P],
                                               rspread[:, qt * P:(qt + 1) * P], ident[:, :])
                last.then_inc(trans_done, 1)

            def out_job(ph, b, tt, rep, k, parts=range(KT)):
                if 0 in parts:
                    bank_free(ph, rep, k)
                    if tt == 0:
                        weights_ready(ph, 3)
                        pe.wait_ge(ctx_lo_done, b * NG + (ph.base["group"] + NG))
                t = slice(tt * P, (tt + 1) * P)
                for kt in parts:
                    last = three(job_bank_of(k)[:, :], (ctxT_hi[:, kt, t], ctxT_lo[:, kt, t]),
                                 (w_hi[:, 3, kt, :], w_lo[:, 3, kt, :]), kt == 0, kt == KT - 1)
                    if kt == KT - 1:
                        last.then_inc(job_done, 1)

            def attention_body(ph, b, to, prev):
                rep, k = start(ph, b, prev)
                dd = freed_dd(ph)
                kp = pro_place(k, prev)
                group3 = ITEMS - TT * G
                for n in range(STEPS):
                    j, i = divmod(n, TT * G)
                    if n < ITEMS:
                        scores(ph, b, n)
                    if 0 <= n - LAG_T < ITEMS:
                        transpose_item(ph, b, n - LAG_T)
                    values(ph, b, n, rep, k)
                    for jj in range(NG):
                        if n == rb_step(jj):
                            reciprocals(ph, b, jj)
                    for tt in range(TT):
                        parts = [kt for kt in range(KT) if n == OUT_AT[KT * tt + kt]]
                        if prev and parts:
                            out_job(ph, b - 1, tt, rep, k + 2 + tt, parts)
                    for jj in range(1, NG + 1):
                        for which in range(2):
                            parts = [part for part in range(KT) if n == qk_at(jj, which)[part]]
                            if not parts or (jj == NG and not to[0].attention):
                                continue
                            kq = qk_place(k, prev, jj, which) if jj < NG else kp + to[0].tiles + which
                            if 0 in parts:
                                if jj == NG:
                                    if which == 0:
                                        y_ready(*to)
                                    else:
                                        pe.wait_ge(job_freed, rep + (kp + to[0].tiles + dd))
                                    if to[0] is not ph:
                                        weights_ready(to[0], which)
                                bank_free(ph, rep, kq)
                            if jj < NG:
                                qk_job(ph, jj, which, kq, parts)
                            else:
                                qk_job(to[0], 0, which, kq, parts)
                    for tile in range(to[0].tiles):
                        if n == TILE_AT[tile]:
                            bank_free(ph, rep, kp + tile)
                            prologue_tile(*to, tile, job_bank_of(kp + tile))
                    for tt in range(TT):
                        if to[0].attention and n == V_AT[tt]:
                            if to[0] is not ph:
                                weights_ready(to[0], 2)
                            kv = kp + to[0].tiles + 2 + tt
                            bank_free(ph, rep, kv)
                            v_job(to[0], tt, kv)
                if to[0] is not ph:
                    for tt in range(TT):
                        out_job(ph, b, tt, rep, out_place(k, to, prev) + tt)

            def mlp_body(ph, b, to, opens):
                rep, k = start(ph, b)
                order = mlp_order(to)
                y_ready(ph, b)
                for l, (kind, n) in enumerate(order):
                    by_act, freed = mlp_freed(ph, b, order, mlp_bank_before(order, l))
                    pe.wait_ge(job_freed_act if by_act else job_freed, freed)
                    dst = mlp_bank(order, l)
                    if kind == "up":
                        if n % KT == 0:
                            weights_ready(ph, n // KT)
                        c = slice((n % KT) * P, (n % KT + 1) * P)
                        for kt in range(KT):
                            end = three(dst[:, :], (w_hi[:, n // KT, kt, c], w_lo[:, n // KT, kt, c]),
                                        (yT_hi[:, kt, :], yT_lo[:, kt, :]), kt == 0, kt == KT - 1)
                        end.then_inc(job_done, 1)
                    elif kind == "tile":
                        prologue_tile(*to, n, dst)
                    elif kind == "down":
                        t = slice(n * P, (n + 1) * P)
                        for m in range(UP):
                            if n == 0 and m % KT == 0:
                                weights_ready(ph, 2 + m // KT)
                            if n == 0:
                                pe.wait_ge(h_lo_done, b * UP + (ph.base["h"] + m + 1))
                            end = three(dst[:, :], (hT_hi[:, m, t], hT_lo[:, m, t]),
                                        (w_hi[:, 2 + m // KT, m % KT, :], w_lo[:, 2 + m // KT, m % KT, :]),
                                        m == 0, m == UP - 1)
                        end.then_inc(job_done, 1)
                    elif kind == "v":
                        weights_ready(to[0], 2)
                        v_job(to[0], n, k + l)
                    else:
                        if n == 0:
                            y_ready(*to)
                        if n == 1:
                            pe.wait_ge(job_freed, mlp_freed(ph, b, order, order.index(("tile", to[0].tiles - 1)))[1])
                        weights_ready(to[0], n)
                        qk_job(to[0], 0, n, k + l)

            pe.wait_ge(const_done, 3)
            pe.wait_ge(vec_loaded, 16 * len(vec_names))
            nc.tensor.transpose(av_bank[0][:, 0:vec_cols], vec_rows, ident[0:vec_cols, 0:vec_cols]).then_inc(vec_turned, 1)
            first = phases[0]
            for tile in range(first.tiles):
                bank_free(first, 0, tile)
                prologue_tile(first, 0, tile, job_bank_of(tile))
            y_ready(first, 0)
            for job in range(2 + TT):
                weights_ready(first, min(job, 2))
                bank_free(first, 0, first.tiles + job)
                if job < 2:
                    qk_job(first, 0, job, first.tiles + job)
                else:
                    v_job(first, job - 2, first.tiles + job)
            for ph in phases:
                bodies(pe, ph, attention_body if ph.attention else mlp_body)

        @block.vector
        def _(dve):
            def ln_moments(ph, b, t):
                s = t % 2
                n = b * TT + (ph.base["tile_ln"] + t + 1)
                dve.wait_ge(x_loaded[s], 16 * (b * (ph.tiles // 2) + (ph.base[f"x{s}"] + t // 2 + 1)))
                nc.vector.bn_stats(stats[:, s, :], xin[:, s, :]).then_inc(ln_stats, 1)
                dve.wait_ge(ln_stats, n)
                alone(dve, dve_held)
                nc.vector.bn_aggr(moments[:, s, :], stats[:, s, :]).then_inc(ln_mom, 1)

            def ln_normalise(ph, b, t):
                s = t % 2
                dve.wait_ge(ln_rstd, b * TT + (ph.base["tile_ln"] + t + 1))
                nc.vector.tensor_scalar(xin[:, s, :], xin[:, s, :], moments[:, s, 0:1], rstd[:, s, 1:2],
                                        ALU.subtract, ALU.mult).then_inc(ln_norm, 1)

            def ln_scale(ph, b, t, done, bank_, y32):
                dve.wait_ge(job_done, done)
                if t >= 2:
                    dve.wait_ge(y_lo_done, b * TT + (ph.base["tile_ln"] + t - 1))
                for ft in range(KT):
                    op = nc.vector.tensor_scalar(y32[:, t % 2, ft, :], bank_[:, ft * P:(ft + 1) * P],
                                                 vec(ph.ln[0], ft), vec(ph.ln[1], ft), ALU.mult, ALU.add)
                op.then_inc(job_freed, 1)

            def enc_low(ph, b, t, bank_):
                dve.wait_ge(enc_hi_done, b * TT + (ph.base["enc"] + t + 1))
                ts = slice(t * P, (t + 1) * P)
                nc.vector.tensor_tensor(encT_lo[:, :, ts], bank_[:, :].rearrange("p (k q) -> p k q", q=P),
                                        encT_hi[:, :, ts].bitcast(f32), ALU.subtract).then_inc(job_freed, 1)

            def qk_low(ph, b, j, which, k):
                name, c = (ph.bq, ph.bk)[which]
                dve.wait_ge(qk_hi_done, 2 * (b * NG + (ph.base["qk"] + j)) + (which + 1))
                nc.vector.scalar_tensor_tensor(out=qk_lo[:, which, :], in0=job_bank_of(k)[:, :], scalar=vec(name, c + j),
                                               in1=qk_hi[:, which, :].bitcast(f32), op0=ALU.add, op1=ALU.subtract)\
                    .then_inc(job_freed, 1)

            def v_copy(tt, rep, k, reader=None):
                dve.wait_ge(job_done, rep + (k + 1))
                if reader:
                    dve.wait_ge(av_done, reader[1] * ITEMS + (reader[0].base["item"] + ITEMS))
                nc.vector.tensor_copy(v_sb[:, tt, :], job_bank_of(k)[:, :]).then_inc(job_freed, 1)

            def front(ph, b, n):
                item = b * ITEMS + ph.base["item"]
                m_done = ph.base["mask"]
                qt = n // G % TT
                if ph.kind == "keys":
                    if n >= ITEMS:
                        return
                    dve.wait_ge(scores_done, item + (n + 1))
                    if n >= U_RING:
                        dve.wait_ge(trans_done, b * (ITEMS + NG) + (ph.base["tentry"] + t_entry(n - U_RING) + 1))
                    if n == 0:
                        dve.wait_ge(w_lo_done, ph.base["weight"] + PIECES)
                        dve.wait_ge(mask_done, b + (m_done + 1))
                    alone(dve, dve_held)
                    nc.vector.tensor_tensor_reduce(out=probs[:, n % U_RING, :], in0=score_bank[n % S_BANKS][:, :],
                                                   in1=maskadd[:, 0, :], scale=-SCALE, scalar=3.0e38, op0=ALU.add,
                                                   op1=ALU.min, accum_out=rowmin[:, n:n + 1]).then_inc(rowmin_done, 1)
                    return
                if n < ITEMS:
                    dve.wait_ge(scores_done, item + (n + 1))
                    if n >= U_RING:
                        dve.wait_ge(trans_done, b * (ITEMS + NG) + (ph.base["tentry"] + t_entry(n - U_RING) + 1))
                    if n == 0:
                        dve.wait_ge(w_lo_done, ph.base["weight"] + PIECES)
                        dve.wait_ge(mask_done, m_done + TT if ph.kind == "self" else b * TT + (m_done + TT))
                    if n >= 1:
                        dve.wait_ge(scores_read, item + n)
                    nc.vector.scalar_tensor_tensor(out=probs[:, n % U_RING, :], in0=score_bank[n % S_BANKS][:, :],
                                                   scalar=-SCALE, in1=mask[:, qt, :], op0=ALU.mult, op1=ALU.mult)\
                        .then_inc(scores_read, 1)
                if 1 <= n <= ITEMS:
                    m = n - 1
                    if n == ITEMS:
                        dve.wait_ge(scores_read, item + ITEMS)
                        alone(dve, dve_held)
                    nc.vector.tensor_tensor_reduce(out=probs[:, m % U_RING, :], in0=probs[:, m % U_RING, :],
                                                   in1=maskadd[:, m // G % TT, :], scale=1.0, scalar=3.0e38,
                                                   op0=ALU.add, op1=ALU.min, accum_out=rowmin[:, m:m + 1])\
                        .then_inc(rowmin_done, 1)

            def invert(ph, b, j):
                dve.wait_ge(exp_done, b * ITEMS + (ph.base["item"] + (j + 1) * TT * G))
                if j >= 1:
                    dve.wait_ge(rspread_done, b * NG + (ph.base["group"] + j))
                nc.vector.reciprocal(rinv[:, :], rowsum[:, j * TT * G:(j + 1) * TT * G]).then_inc(rinv_done, 1)

            def normalise(ph, b, j):
                dve.wait_ge(trans_read, b * (ITEMS + NG) + (ph.base["tentry"] + rb_entry(j) + 1))
                dve.wait_ge(av_done, b * ITEMS + (ph.base["item"] + TT * G * (j + 1)))
                nc.vector.tensor_tensor(ctx32[:, :], av_bank[j % 2][:, :], ctx32[:, :], ALU.mult).then_inc(ctx_done, 1)

            def ctx_low(ph, b, j):
                name, c = ph.bv
                dve.wait_ge(ctx_hi_done, b * NG + (ph.base["group"] + j + 1))
                nc.vector.scalar_tensor_tensor(out=ctxT_lo[:, j, :], in0=ctx32[:, :], scalar=vec(name, c + j),
                                               in1=ctxT_hi[:, j, :].bitcast(f32), op0=ALU.add, op1=ALU.subtract)\
                    .then_inc(ctx_lo_done, 1)

            def add_residual(ph, b, tt, done, k):
                dve.wait_ge(job_done, done)
                if ph.out_bias:
                    dve.wait_ge(res_biased, b * TT + (ph.base["bias"] * B * TT + tt + 1))
                else:
                    dve.wait_ge(res_loaded[tt % ph.res_slots], res_count(ph, b, tt, "res", 1))
                nc.vector.tensor_tensor(res_tile(ph, tt), job_bank_of(k)[:, :], res_tile(ph, tt), ALU.add).then_inc(job_freed, 1)

            def mask_part(to, qt):
                dve.wait_ge(mask_loaded[qt], 16 * (to[1] + (to[0].base["mask"] // TT + 1)))
                nc.vector.tensor_scalar(maskadd[:, qt, :], mask[:, qt, :], 1.0, -10000.0, ALU.subtract, ALU.mult)\
                    .then_inc(mask_done, 1)

            def keys_part(to):
                dve.wait_ge(mask_loaded[TT - 1], 16 * (to[1] + (to[0].base["mask"] // TT + 1)))
                nc.vector.tensor_scalar(maskadd[:, 0, :], mask_u8, 1.0, MASKED, ALU.subtract, ALU.mult)\
                    .then_inc(mask_done, 1)

            def hidden_low(ph, b, m):
                dve.wait_ge(h_hi_done, b * UP + (ph.base["h"] + m + 1))
                nc.vector.tensor_tensor(hT_lo[:, m, :], h32[:, m % 3, :, :].rearrange("p k q -> p (k q)"),
                                        hT_hi[:, m, :].bitcast(f32), ALU.subtract).then_inc(h_lo_done, 1)

            def attention_body(ph, b, to, prev):
                rep, k = start(ph, b, prev)
                kp = pro_place(k, prev)
                group3 = ITEMS - TT * G
                for n in range(STEPS):
                    j, i = divmod(n, TT * G)
                    front(ph, b, n)
                    for tt in range(TT):
                        if prev and n == OUT_AT[KT * tt + KT - 1] + 2:
                            add_residual(ph, b - 1, tt, rep + (k + 2 + tt + 1), k + 2 + tt)
                    for which in range(2):
                        for jj in range(1, NG):
                            if n == qk_at(jj, which)[-1] + 2:
                                qk_low(ph, b, jj, which, qk_place(k, prev, jj, which))
                        if to[0].attention and n == qk_at(NG, which)[-1] + 2:
                            qk_low(*to, 0, which, kp + to[0].tiles + which)
                    for jj in range(NG):
                        if n == rb_step(jj) - 2:
                            invert(ph, b, jj)
                        if n == norm_step(jj):
                            normalise(ph, b, jj)
                        if n == norm_step(jj) + 1:
                            ctx_low(ph, b, jj)
                    for t in range(TT):
                        if n == LN_AT[t]:
                            ln_moments(*to, t)
                        if n == LN_AT[t] + 2:
                            ln_normalise(*to, t)
                        if n == LN_AT[t] + 4:
                            ln_scale(*to, t, rep + (kp + t + 1), job_bank_of(kp + t), y32_of[True])
                        if to[0].cross and n == TILE_AT[TT + t] + 1:
                            enc_low(*to, t, job_bank_of(kp + TT + t))
                        if to[0].kind == "cross" and n == group3 + G * t + 9:
                            dve.wait_ge(rowmin_done, b * ITEMS + (ph.base["item"] + group3 + G * (t + 1)))
                            mask_part(to, t)
                    if to[0].kind == "keys" and n == ITEMS:
                        dve.wait_ge(rowmin_done, b * ITEMS + (ph.base["item"] + ITEMS))
                        keys_part(to)
                    for tt in range(TT):
                        if to[0].attention and n == min(V_AT[tt] + 2, STEPS - 1):
                            v_copy(tt, rep, kp + to[0].tiles + 2 + tt, (ph, b))
                if to[0] is not ph:
                    ko = out_place(k, to, prev)
                    for tt in range(TT):
                        add_residual(ph, b, tt, rep + (ko + tt + 1), ko + tt)

            def mlp_body(ph, b, to, opens):
                rep, k = start(ph, b)
                order = mlp_order(to)

                def place(job):
                    return k + order.index(job)

                def down(tt):
                    kk = place(("down", tt))
                    add_residual(ph, b, tt, rep + (kk + 1), kk)

                if to:
                    for t in range(2):
                        ln_moments(*to, t)
                        ln_normalise(*to, t)
                    if to[0].kind == "keys":
                        keys_part(to)
                for m in range(UP):
                    hidden_low(ph, b, m)
                for half in range(2):
                    pair = (2 * half, 2 * half + 1)
                    if to:
                        for t in pair:
                            kk = place(("tile", t))
                            ln_scale(*to, t, rep + (kk + 1), score_bank[t % 2], y32_of[False])
                        if half == 0:
                            for t in (2, 3):
                                ln_moments(*to, t)
                                ln_normalise(*to, t)
                    for tt in pair:
                        down(tt)
                if to and to[0].cross:
                    for t in range(TT):
                        enc_low(*to, t, score_bank[t % 2])
                    for which in range(2):
                        qk_low(*to, 0, which, place(("qk", which)))
                    for tt in range(TT):
                        v_copy(tt, rep, place(("v", tt)))

            dve.wait_ge(vec_turned, 1)
            nc.vector.tensor_copy(vecs[:, :], av_bank[0][:, 0:vec_cols]).then_inc(vec_done, 1)
            dve.wait_ge(vec_done, 1)
            first = phases[0]
            for t in range(TT):
                ln_moments(first, 0, t)
                ln_normalise(first, 0, t)
                ln_scale(first, 0, t, t + 1, job_bank_of(t), y32_of[True])
            for qt in range(TT):
                mask_part((first, 0), qt)
            for which in range(2):
                qk_low(first, 0, 0, which, first.tiles + which)
            for tt in range(TT):
                v_copy(tt, 0, first.tiles + 2 + tt)
            for ph in phases:
                bodies(dve, ph, attention_body if ph.attention else mlp_body)

        @block.scalar
        def _(act):
            def y_high(ph, b, t, freed, y32):
                act.wait_ge(job_freed, freed)
                nc.scalar.activation(yT_hi[:, :, t * P:(t + 1) * P], y32[:, t % 2, :, :], ACT.Copy).then_inc(y_hi_done, 1)

            def enc_high(ph, b, t, rep, k, bank_):
                act.wait_ge(job_done, rep + (k + 1))
                nc.scalar.activation(encT_hi[:, :, t * P:(t + 1) * P],
                                     bank_[:, :].rearrange("p (k q) -> p k q", q=P), ACT.Copy)\
                    .then_inc(enc_hi_done, 1)

            def qk_high(ph, b, j, which, rep, k):
                name, c = (ph.bq, ph.bk)[which]
                act.wait_ge(job_done, rep + (k + 1))
                ge(act, stacked[which], 16 * 3 * G * (b * NG + (ph.base["qk"] + j)))
                nc.scalar.activation(qk_hi[:, which, :], job_bank_of(k)[:, :], ACT.Identity, bias=vec(name, c + j))\
                    .then_inc(qk_hi_done, 1)

            def exponent(ph, b, n):
                act.wait_ge(rowmin_done, b * ITEMS + (ph.base["item"] + n + 1))
                nc.scalar.activation(probs[:, n % U_RING, :], probs[:, n % U_RING, :], ACT.Exp, bias=rowmin[:, n:n + 1],
                                     scale=-1.0, accum_out=rowsum[:, n:n + 1]).then_inc(exp_done, 1)

            def copy_item(ph, b, n):
                e = t_entry(n)
                act.wait_ge(trans_done, b * (ITEMS + NG) + (ph.base["tentry"] + e + 1))
                if n >= PT_RING:
                    act.wait_ge(av_done, b * ITEMS + (ph.base["item"] + n - PT_RING + 1))
                nc.scalar.activation(pT[:, n % PT_RING, :, :].rearrange("p k q -> p (k q)"), trans_bank[e % T_BANKS][:, :],
                                     ACT.Copy).then_inc(trans_read, 1)

            def copy_reciprocals(ph, b, j):
                e = rb_entry(j)
                act.wait_ge(trans_done, b * (ITEMS + NG) + (ph.base["tentry"] + e + 1))
                if j >= 1:
                    act.wait_ge(ctx_lo_done, b * NG + (ph.base["group"] + j))
                nc.scalar.activation(ctx32[:, :], trans_bank[e % T_BANKS][:, :], ACT.Copy).then_inc(trans_read, 1)

            def ctx_high(ph, b, j):
                name, c = ph.bv
                act.wait_ge(ctx_done, b * NG + (ph.base["group"] + j + 1))
                nc.scalar.activation(ctxT_hi[:, j, :], ctx32[:, :], ACT.Identity, bias=vec(name, c + j))\
                    .then_inc(ctx_hi_done, 1)

            def weight_fetch(ph, piece):
                slot, kt = divmod(piece, KT)
                if piece >= RAW:
                    act.wait_ge(w_lo_done, ph.base["weight"] + piece - RAW + 1)
                act.dma_start(raw_of(ph, piece), ph.weights[slot](kt)).then_inc(w_loaded[piece % RAW], 16)

            def weight_high(ph, piece, upto):
                slot, kt = divmod(piece, KT)
                if piece + RAW - 1 < upto:
                    weight_fetch(ph, piece + RAW - 1)
                act.wait_ge(w_loaded[piece % RAW], 16 * ((ph.base["weight"] + piece) // RAW + 1))
                nc.scalar.activation(w_hi[:, slot, kt, :], raw_of(ph, piece), ACT.Copy).then_inc(w_hi_done, 1)

            def weight_run(ph, first, upto):
                for piece in range(first, min(first + RAW - 1, upto)):
                    weight_fetch(ph, piece)
                for piece in range(first, upto):
                    weight_high(ph, piece, upto)

            def attention_body(ph, b, to, prev):
                rep, k = start(ph, b, prev)
                kp = pro_place(k, prev)
                dd = freed_dd(ph)
                group3 = ITEMS - TT * G
                fresh = to[0] is not ph
                for n in range(STEPS):
                    j, i = divmod(n, TT * G)
                    for jj in range(NG):
                        if n == rb_step(jj) + 1:
                            copy_reciprocals(ph, b, jj)
                    m = n - LAG_T
                    if 0 <= m < ITEMS:
                        copy_item(ph, b, m)
                    if 1 <= n <= ITEMS:
                        exponent(ph, b, n - 1)
                    for jj in range(NG):
                        if n == norm_step(jj):
                            ctx_high(ph, b, jj)
                    if fresh and n == PREFETCH:
                        act.wait_ge(job_done, rep + kp)
                        for which in range(2):
                            act.wait_ge(stacked[which], 16 * 3 * G * (ph.base["qk"] + B * NG))
                        for piece in range(RAW - 1):
                            weight_fetch(to[0], piece)
                    if fresh and 0 <= n - PREFETCH < 3 * KT:
                        weight_high(to[0], n - PREFETCH, 3 * KT)
                    for which in range(2):
                        for jj in range(1, NG):
                            if n == qk_at(jj, which)[-1] + 1:
                                qk_high(ph, b, jj, which, rep, qk_place(k, prev, jj, which))
                        if to[0].attention and n == qk_at(NG, which)[-1] + 1:
                            if fresh:
                                act.wait_ge(w_lo_done, to[0].base["weight"] + 3 * KT)
                            qk_high(*to, 0, which, rep, kp + to[0].tiles + which)
                    for t in range(TT):
                        if n == LN_AT[t] + 4:
                            y_high(*to, t, rep + (kp + t + 1 + dd), y32_of[True])
                        if to[0].cross and n == TILE_AT[TT + t]:
                            enc_high(*to, t, rep, kp + TT + t, job_bank_of(kp + TT + t))
                if fresh and late_from(to[0]) == PIECES:
                    act.wait_ge(job_done, rep + (out_place(k, to, prev) + TT))
                    weight_run(to[0], 3 * KT, PIECES)

            def mlp_body(ph, b, to, opens):
                rep, k = start(ph, b)
                order = mlp_order(to)
                fresh = to and to[0] is not ph

                def hidden_high(m):
                    act.wait_ge(job_freed_act, b * UP + (ph.base["afree"] + m + 1))
                    nc.scalar.activation(hT_hi[:, m, :], h32[:, m % 3, :, :].rearrange("p k q -> p (k q)"), ACT.Copy)\
                        .then_inc(h_hi_done, 1)

                late = late_from(ph)
                if opens:
                    act.wait_ge(job_done, k)
                    for piece in range(late, late + RAW - 1):
                        weight_fetch(ph, piece)
                for m in range(UP):
                    act.wait_ge(job_done, rep + (k + m + 1))
                    if m >= 3:
                        act.wait_ge(h_lo_done, b * UP + (ph.base["h"] + m - 2))
                    nc.scalar.activation(h32[:, m % 3, :, :].rearrange("p k q -> p (k q)"), job_bank_of(k + m)[:, :],
                                         ACT.Gelu_apprx_tanh, bias=vec(ph.b1, ph.half * UP + m)).then_inc(job_freed_act, 1)
                    if m >= 1:
                        hidden_high(m - 1)
                    if opens and late + m < PIECES:
                        weight_high(ph, late + m, PIECES)
                hidden_high(UP - 1)
                for half in range(2):
                    if to:
                        for t in (2 * half, 2 * half + 1):
                            y_high(*to, t, mlp_freed(ph, b, order, order.index(("tile", t)))[1], y32_of[False])
                    if fresh:
                        weight_run(to[0], half * KT, (half + 1) * KT)
                if fresh:
                    if to[0].cross:
                        for t in range(TT):
                            enc_high(*to, t, rep, k + order.index(("tile", TT + t)), score_bank[t % 2])
                    if to[0].attention:
                        act.wait_ge(job_done, rep + (k + order.index(("down", 3)) + 1))
                        weight_run(to[0], 2 * KT, 3 * KT)
                        for which in range(2):
                            qk_high(*to, 0, which, rep, k + order.index(("qk", which)))
                        weight_run(to[0], 3 * KT, PIECES)

            first = phases[0]
            weight_run(first, 0, KT)
            act.wait_ge(vec_done, 1)
            for t in range(TT):
                y_high(first, 0, t, t + 1, y32_of[True])
                if t != 2:
                    slot = t + 1 if t < 2 else t
                    weight_run(first, slot * KT, (slot + 1) * KT)
            for which in range(2):
                qk_high(first, 0, 0, which, 0, first.tiles + which)
            for ph in phases:
                bodies(act, ph, attention_body if ph.attention else mlp_body)


_INS = ['x', 'ctx_2048', 'mask_1x1xSxS2_fc1', 'mask_Bx1xSxS2_ff1', 'mask_BxS2_bf1',
        'L0_xattn_ln1_s', 'L0_xattn_ln1_b', 'L0_xattn_w_qkv', 'L0_xattn_b_qkv', 'L0_xattn_w_ao', 'L0_xattn_b_ao',
        'L0_xattn_ln2_s', 'L0_xattn_ln2_b', 'L0_xattn_w_q', 'L0_xattn_b_q', 'L0_xattn_w_kv', 'L0_xattn_b_kv',
        'L0_xattn_w_co', 'L0_xattn_b_co', 'L0_xattn_ln3_s', 'L0_xattn_ln3_b', 'L0_xattn_w1', 'L0_xattn_b1',
        'L0_xattn_w2', 'L0_xattn_b2', 'L1_xattn_ln1_w', 'L1_xattn_ln1_b', 'L1_xattn_q_w', 'L1_xattn_q_b',
        'L1_xattn_k_w', 'L1_xattn_k_b', 'L1_xattn_v_w', 'L1_xattn_v_b', 'L1_xattn_cproj_w', 'L1_xattn_cproj_b',
        'L1_xattn_ln2_w', 'L1_xattn_ln2_b', 'L1_xattn_fc_w', 'L1_xattn_fc_b', 'L1_xattn_proj_w', 'L1_xattn_proj_b']


def kernel(**inputs):
    import numpy as _np
    import concourse.bacc as _bacc
    from concourse import mybir as _mybir
    from concourse.bass_utils import run_bass_kernel_spmd as _run

    nc = _bacc.Bacc("TRN2", target_bir_lowering=False, num_devices=1)
    arrays, aps = {}, {}
    for name in _INS:
        a = _np.ascontiguousarray(inputs[name])
        arrays[f"in_{name}"] = a
        aps[name] = nc.dram_tensor(f"in_{name}", a.shape, _mybir.dt.from_np(a.dtype), kind="ExternalInput").ap()
    out = nc.dram_tensor("out_0", (B, S, D), _mybir.dt.float32, kind="ExternalOutput").ap()
    xattn_program(nc, aps, out)
    r = _run(nc, [arrays], core_ids=[0])
    return r.results[0]["out_0"]
```
